# Optimizing a Trainium2 kernel written in Bass

```python
import numpy as np
import jax
import jax.numpy as jnp

def _softmax(x, axis=-1):
    return jax.nn.softmax(x, axis=axis)

def _gelu(x):
    return jax.nn.gelu(x, approximate=True)

def _silu(x):
    return jax.nn.silu(x)

def _sigmoid(x):
    return jax.nn.sigmoid(x)

def _layernorm(x, axis=-1, eps=1e-05):
    m = jnp.mean(x, axis=axis, keepdims=True)
    v = jnp.var(x, axis=axis, keepdims=True)
    return (x - m) / jnp.sqrt(v + eps)

def _scatter_add(tgt, idx, src, axis=0):
    return tgt.at[idx].add(src)

def _segment_sum(src, seg, n):
    return jax.ops.segment_sum(src, seg, n)
kernel_name = 'mk_adj_resnorm_d4_adj_r2_f11c4b'

def setup_inputs(seed: int=0):
    np.random.seed(seed)
    _w = jnp.asarray

    def _rec_inputs():
        import jax
        import jax.numpy as jnp
        _gk = jax.random.key(seed)
        x = -0.003407 + 1.001 * jax.random.normal(jax.random.fold_in(_gk, 1), (8, 1024, 64), jnp.float32)
        _w = (1.0 + jnp.arange(1024, dtype=jnp.float32)) ** (-0.5)
        _w = _w / _w.mean()
        _pij = jnp.clip(0.00390625 * _w[:, None] * _w[None, :], 0.0, 1.0)
        _a = jax.random.uniform(jax.random.fold_in(_gk, 2), (8, 1024, 1024)) < _pij
        _a = jnp.logical_or(_a, jnp.swapaxes(_a, -1, -2))
        _a = jnp.logical_or(_a, jnp.eye(1024, dtype=bool))
        _af = _a.astype(jnp.float32)
        _af = _af * jax.random.uniform(jax.random.fold_in(_gk, 3), (8, 1024, 1024), jnp.float32, 0.05, 0.999994)
        adj = _af
        _nm = jnp.ones((8, 1024), dtype=bool)
        nodemask = jnp.where(_nm, 1.0, 0.0).astype(jnp.float32)
        return (x, adj, nodemask)
    x, adj, nodemask = _rec_inputs()

    def _L0_gnn_setup():
        import jax, jax.numpy as jnp
        import numpy as np
        B, N, H = (4, 256, 64)
        key = jax.random.key(seed)
        ks = jax.random.split(key, 11)
        s = 0.05
        return {'t': jnp.float32(0.5), 'h': jax.random.normal(ks[0], (B, N, H), dtype=jnp.float32), 'adjacency': jax.random.uniform(ks[1], (B, N, N), dtype=jnp.float32), 'W1': jax.random.normal(ks[2], (2 * H, H), dtype=jnp.float32) * s, 'b1': jax.random.normal(ks[3], (H,), dtype=jnp.float32) * s, 'W2': jax.random.normal(ks[4], (H, H), dtype=jnp.float32) * s, 'b2': jax.random.normal(ks[5], (H,), dtype=jnp.float32) * s, 'E1': jax.random.normal(ks[6], (2 * H, H), dtype=jnp.float32) * s, 'be1': jax.random.normal(ks[7], (H,), dtype=jnp.float32) * s, 'E2': jax.random.normal(ks[8], (H, 1), dtype=jnp.float32) * s, 'be2': jax.random.normal(ks[9], (1,), dtype=jnp.float32) * s}
    _L0_gnn_all = _L0_gnn_setup()
    _L0_gnn_in = {k: v for k, v in _L0_gnn_all.items() if k in ('t', 'W1', 'b1', 'W2', 'b2', 'E1', 'be1', 'E2', 'be2')}
    del _L0_gnn_all

    def _L1_gnn_setup():
        import jax, jax.numpy as jnp
        import numpy as np
        key = jax.random.key(seed)
        k1, k2, k3, k4 = jax.random.split(key, 4)
        B, N, F_in, F_out = (8, 2048, 64, 64)
        stdv = 1.0 / np.sqrt(F_out)
        inputs = jax.random.normal(k1, (B, N, F_in), dtype=jnp.float32)
        adj = jax.random.uniform(k2, (B, N, N), dtype=jnp.float32)
        weight = jax.random.uniform(k3, (F_in, F_out), minval=-stdv, maxval=stdv, dtype=jnp.float32)
        bias = jax.random.uniform(k4, (F_out,), minval=-stdv, maxval=stdv, dtype=jnp.float32)
        return {'input': inputs, 'adj': adj, 'weight': weight, 'bias': bias}
    _L1_gnn_all = _L1_gnn_setup()
    _L1_gnn_in = {k: v for k, v in _L1_gnn_all.items() if k in ('weight', 'bias')}
    del _L1_gnn_all

    def _L2_gnn_setup():
        import jax, jax.numpy as jnp
        import numpy as np
        NUM_LAYERS = 3
        IN_DIM, HID, LAT = (64, 128, 32)
        B, N = (32, 512)
        NORM_FACTOR = 1.0
        key = jax.random.key(seed)
        ks = jax.random.split(key, 8)
        x = jax.random.normal(ks[0], (B, N, IN_DIM), dtype=jnp.float32)
        adj = jax.random.uniform(ks[1], (B, N, N), dtype=jnp.float32)
        node_mask = jnp.ones((B, N, 1), dtype=jnp.float32)
        s_in = 1.0 / np.sqrt(IN_DIM)
        s_h = 1.0 / np.sqrt(HID)
        W_embed = jax.random.uniform(ks[2], (IN_DIM, HID), jnp.float32, -s_in, s_in)
        Wl = jax.random.uniform(ks[3], (NUM_LAYERS, HID, HID), jnp.float32, -s_h, s_h)
        bl = jax.random.uniform(ks[4], (NUM_LAYERS, HID), jnp.float32, -s_h, s_h)
        W_proj = jax.random.uniform(ks[5], (HID, 2 * LAT), jnp.float32, -s_h, s_h)
        b_proj = jax.random.uniform(ks[6], (2 * LAT,), jnp.float32, -s_h, s_h)
        return {'node_features': x, 'adjacency_matrix': adj, 'node_mask': node_mask, 'W_embed': W_embed, 'Wl': Wl, 'bl': bl, 'W_proj': W_proj, 'b_proj': b_proj}
    _L2_gnn_all = _L2_gnn_setup()
    _L2_gnn_in = {k: v for k, v in _L2_gnn_all.items() if k in ('W_embed', 'Wl', 'bl', 'W_proj', 'b_proj')}
    del _L2_gnn_all

    def _L3_gnn_setup():
        import jax, jax.numpy as jnp
        import numpy as np
        NORM = 1.0

        def _glorot(key, shape):
            fan_in, fan_out = shape
            lim = float(np.sqrt(6.0 / (fan_in + fan_out)))
            return jax.random.uniform(key, shape, jnp.float32, -lim, lim)

        def _gcn_layer(h, adj, W, b):
            msg = h @ W + b
            agg = jnp.einsum('bij,bjd->bid', adj, msg) / NORM
            return jax.nn.relu(agg)
        key = jax.random.key(seed)
        ks = jax.random.split(key, 12)
        B, N = (8, 1024)
        latent, hidden, out_dim = (64, 128, 64)
        inp = {'latent_features': jax.random.normal(ks[0], (B, N, latent), jnp.float32), 'adjacency_matrix': jax.random.uniform(ks[1], (B, N, N), jnp.float32), 'node_mask': jnp.ones((B, N, 1), jnp.float32), 'W0': _glorot(ks[2], (latent, hidden)), 'b0': jnp.zeros((hidden,), jnp.float32), 'W1': _glorot(ks[3], (hidden, hidden)), 'b1': jnp.zeros((hidden,), jnp.float32), 'W2': _glorot(ks[4], (hidden, hidden)), 'b2': jnp.zeros((hidden,), jnp.float32), 'Wout': _glorot(ks[5], (hidden, out_dim)), 'bout': jnp.zeros((out_dim,), jnp.float32)}
        return inp
    _L3_gnn_all = _L3_gnn_setup()
    _L3_gnn_in = {k: v for k, v in _L3_gnn_all.items() if k in ('W0', 'b0', 'W1', 'b1', 'W2', 'b2', 'Wout', 'bout')}
    del _L3_gnn_all
    return {'x': x, 'adj': adj, 'nodemask': nodemask, 'L0_gnn_t': _L0_gnn_in['t'], 'L0_gnn_W1': _L0_gnn_in['W1'], 'L0_gnn_b1': _L0_gnn_in['b1'], 'L0_gnn_W2': _L0_gnn_in['W2'], 'L0_gnn_b2': _L0_gnn_in['b2'], 'L0_gnn_E1': _L0_gnn_in['E1'], 'L0_gnn_be1': _L0_gnn_in['be1'], 'L0_gnn_E2': _L0_gnn_in['E2'], 'L0_gnn_be2': _L0_gnn_in['be2'], 'L1_gnn_weight': _L1_gnn_in['weight'], 'L1_gnn_bias': _L1_gnn_in['bias'], 'L2_gnn_W_embed': _L2_gnn_in['W_embed'], 'L2_gnn_Wl': _L2_gnn_in['Wl'], 'L2_gnn_bl': _L2_gnn_in['bl'], 'L2_gnn_W_proj': _L2_gnn_in['W_proj'], 'L2_gnn_b_proj': _L2_gnn_in['b_proj'], 'L3_gnn_W0': _L3_gnn_in['W0'], 'L3_gnn_b0': _L3_gnn_in['b0'], 'L3_gnn_W1': _L3_gnn_in['W1'], 'L3_gnn_b1': _L3_gnn_in['b1'], 'L3_gnn_W2': _L3_gnn_in['W2'], 'L3_gnn_b2': _L3_gnn_in['b2'], 'L3_gnn_Wout': _L3_gnn_in['Wout'], 'L3_gnn_bout': _L3_gnn_in['bout']}

def reference(x, adj, nodemask, L0_gnn_t, L0_gnn_W1, L0_gnn_b1, L0_gnn_W2, L0_gnn_b2, L0_gnn_E1, L0_gnn_be1, L0_gnn_E2, L0_gnn_be2, L1_gnn_weight, L1_gnn_bias, L2_gnn_W_embed, L2_gnn_Wl, L2_gnn_bl, L2_gnn_W_proj, L2_gnn_b_proj, L3_gnn_W0, L3_gnn_b0, L3_gnn_W1, L3_gnn_b1, L3_gnn_W2, L3_gnn_b2, L3_gnn_Wout, L3_gnn_bout):
    import jax
    import jax.numpy as jnp

    def _L0_gnn_ref(t, h, adjacency, W1, b1, W2, b2, E1, be1, E2, be2):
        import jax, jax.numpy as jnp
        import numpy as np
        B, N, H = (4, 256, 64)
        messages = jnp.einsum('bij,bjh->bih', adjacency, h)
        node_in = jnp.concatenate([h, messages], axis=-1)
        dh = jnp.tanh(node_in @ W1 + b1) @ W2 + b2
        hd = h.shape[-1]
        pi = h @ E1[:hd]
        pj = h @ E1[hd:]
        eh = jnp.tanh(pi[:, :, None, :] + pj[:, None, :, :] + be1)
        edge_updates = (eh @ E2)[..., 0] + be2[0]
        _ = adjacency + edge_updates
        return dh

    def _L1_gnn_ref(input, adj, weight, bias):
        import jax, jax.numpy as jnp
        import numpy as np
        support = jnp.einsum('bni,io->bno', input, weight)
        out = jnp.einsum('bnm,bmo->bno', adj, support)
        return out + bias

    def _L2_gnn_ref(node_features, adjacency_matrix, node_mask, W_embed, Wl, bl, W_proj, b_proj):
        import jax, jax.numpy as jnp
        import numpy as np
        NUM_LAYERS = 3
        IN_DIM, HID, LAT = (64, 128, 32)
        B, N = (32, 512)
        NORM_FACTOR = 1.0
        h = jnp.einsum('bni,ih->bnh', node_features, W_embed)
        for i in range(NUM_LAYERS):
            msg = jnp.einsum('bnh,hk->bnk', h, Wl[i]) + bl[i]
            agg = jnp.einsum('bnm,bmk->bnk', adjacency_matrix, msg) / NORM_FACTOR
            h = jax.nn.relu(agg)
        mean_logvar = jnp.einsum('bnh,hk->bnk', h, W_proj) + b_proj
        return mean_logvar * node_mask

    def _L3_gnn_ref(latent_features, adjacency_matrix, node_mask, W0, b0, W1, b1, W2, b2, Wout, bout):
        import jax, jax.numpy as jnp
        import numpy as np
        NORM = 1.0

        def _glorot(key, shape):
            fan_in, fan_out = shape
            lim = float(np.sqrt(6.0 / (fan_in + fan_out)))
            return jax.random.uniform(key, shape, jnp.float32, -lim, lim)

        def _gcn_layer(h, adj, W, b):
            msg = h @ W + b
            agg = jnp.einsum('bij,bjd->bid', adj, msg) / NORM
            return jax.nn.relu(agg)
        h = _gcn_layer(latent_features, adjacency_matrix, W0, b0)
        h = _gcn_layer(h, adjacency_matrix, W1, b1)
        h = _gcn_layer(h, adjacency_matrix, W2, b2)
        return (h @ Wout + bout) * node_mask
    x = _layernorm(x + _L0_gnn_ref(L0_gnn_t, x, adj, L0_gnn_W1, L0_gnn_b1, L0_gnn_W2, L0_gnn_b2, L0_gnn_E1, L0_gnn_be1, L0_gnn_E2, L0_gnn_be2), axis=-1)
    x = _layernorm(x + _L1_gnn_ref(x, adj, L1_gnn_weight, L1_gnn_bias), axis=-1)
    x = _layernorm(x + _L2_gnn_ref(x, adj, nodemask[..., None], L2_gnn_W_embed, L2_gnn_Wl, L2_gnn_bl, L2_gnn_W_proj, L2_gnn_b_proj), axis=-1)
    x = _layernorm(x + _L3_gnn_ref(x, adj, nodemask[..., None], L3_gnn_W0, L3_gnn_b0, L3_gnn_W1, L3_gnn_b1, L3_gnn_W2, L3_gnn_b2, L3_gnn_Wout, L3_gnn_bout), axis=-1)
    return x

_drawn_inputs = setup_inputs


def setup_inputs(seed=0):
    import zlib

    import numpy as np

    out = dict(_drawn_inputs(seed))
    spreads = {'L3_gnn_b0': (0.0, 0.1),
     'L3_gnn_b1': (0.0, 0.1),
     'L3_gnn_b2': (0.0, 0.8),
     'L3_gnn_bout': (0.0, 0.8)}
    factors = {}
    for name, (base, spread) in spreads.items():
        noise = np.random.default_rng([zlib.crc32(name.encode()), seed]).standard_normal(out[name].shape)
        drawn = base * np.exp(spread * noise) if base else spread * noise
        out[name] = jnp.asarray(drawn.astype(out[name].dtype))
    for name, factor in factors.items():
        out[name] = (out[name] * factor).astype(out[name].dtype)
    return out
```

```python
from contextlib import ExitStack

import numpy as np

import concourse.bass as bass
from concourse import mybir


P = 128
B, N, D, HID = 8, 1024, 64, 128
CH = N // P
HALF = N // 2
HC = CH // 2
PAIRS = B // 2
SLOTS = CH // 2
EPS = 1e-5

F32 = mybir.dt.float32
F32R = mybir.dt.float32r
ALU = mybir.AluOpType
ACT = mybir.ActivationFunctionType
AX_X = mybir.AxisListType.X

EXACT = ["ones", "ident"]
SPLIT = ["w1b", "w1a", "dec0"]
WIDE = ["enc1", "enc2", "dec1", "dec2"]
NARROW = ["w2", "gcn", "proj", "dout"]
N_EXACT = len(EXACT) * P
N_SPLIT = N_EXACT + len(SPLIT) * P
N_WHOLE = len(WIDE) * P + len(NARROW) * D
HI_COL = {n: i * P for i, n in enumerate(EXACT + SPLIT + ["enc0"])}
WHOLE_COL = {n: i * P for i, n in enumerate(WIDE)}
WHOLE_COL |= {n: len(WIDE) * P + i * D for i, n in enumerate(NARROW)}
EMBED, ENC0, N_STAGE = N_SPLIT, N_SPLIT + P, N_SPLIT + 2 * P
BCOL = {"enc1": 0, "enc2": 128, "dec1": 256, "dec2": 384, "w2": 512, "gcn": 576, "proj": 640, "dout": 704,
        "tanh": 768, "enc0": 769, "dec0": 770}
N_BIAS = 771

FIRST_AT, SECOND_AT = 5, 22
XT_AT, X_TERM_AT = 12, 28

LN_OF = {0: 0, 1: 1, 4: 2, 7: 3}
LIFT_OF = {2: 0, 5: 1}
MSG_OF = {2: 0, 3: 1, 5: 2, 6: 3}
LIFT_W = {2: "enc0", 5: "dec0"}
MSG_W = {2: "enc1", 3: "enc2", 5: "dec1", 6: "dec2"}
NODE_W = {1: "gcn", 4: "proj", 7: "dout"}
NARROW_K = (0, 1, 2, 5)
ORDER = [(k, s) for k in range(8) for s in range(2)]
FILLS = [(k, s) for k in (0, 1, 2, 5) for s in range(2)]


def graph_networks(nc: bass.Bass, x, adj_t, mask, weights, whole, biases, out):
    with ExitStack() as ctx:
        def sb(name, shape, dt=F32):
            return ctx.enter_context(nc.sbuf_tensor(name, shape, dt))

        def sem(name):
            return ctx.enter_context(nc.semaphore(name))

        def sems(name, n):
            return [sem(f"{name}{i}") for i in range(n)]

        a_hi = [sb(f"a_hi{s}", [P, CH, N], F32R) for s in range(2)]
        a_lo = [sb(f"a_lo{s}", [P, CH, N], F32R) for s in range(2)]
        raw = sb("raw", [P, CH, N])
        stat = [sb(f"stat{s}", [P, CH, 2 * HID], F32R) for s in range(2)]
        feat_hi = sb("feat_hi", [P, N], F32R)
        feat_lo = sb("feat_lo", [P, N], F32R)
        rows = [sb(f"rows{s}", [P, N]) for s in range(2)]
        work = [sb(f"work{s}", [P, N]) for s in range(2)]
        xn = [sb(f"xn{s}", [P, CH, D]) for s in range(2)]
        x_in = sb("x_in", [P, CH, D])
        spare = sb("spare", [P, CH, D])
        mk = [sb(f"mk{s}", [P, CH]) for s in range(2)]
        w_hi = sb("w_hi", [P, N_SPLIT + P], F32R)
        w_lo = sb("w_lo", [P, N_SPLIT + P - N_EXACT], F32R)
        w_whole = sb("w_whole", [P, N_WHOLE])
        bias = sb("bias", [P, N_BIAS])
        ln_s = sb("ln_s", [P, CH])
        ln_q = sb("ln_q", [P, CH])
        ln_d = sb("ln_d", [P, CH])
        idle = sb("idle", [P, 1])
        ln_r = sb("ln_r", [P, CH])
        eps = sb("eps", [P, 1])
        eps_set = sem("eps_set")
        table_loaded = sem("table_loaded")
        stage_w = raw[:, CH - 2:CH, :].rearrange("p c n -> p (c n)")
        y = [work[s][:, 0:HALF].rearrange("p (c d) -> p c d", d=D) for s in range(2)]
        sq = [work[s][:, HALF:N].rearrange("p (c d) -> p c d", d=D) for s in range(2)]

        agg = [ctx.enter_context(nc.psum_tensor(f"agg{s}", [P, N], F32)) for s in range(2)]
        den = [ctx.enter_context(nc.psum_tensor(f"den{s}", [P, N], F32)) for s in range(2)]

        w_loaded = sem("w_loaded")
        w_rounded = sem("w_rounded")
        w_product = sem("w_product")
        w_ready = sem("w_ready")
        whole_loaded = sem("whole_loaded")
        bias_loaded = sem("bias_loaded")
        x_loaded = sem("x_loaded")
        mask_loaded = sems("mask_loaded", 2)
        raw_loaded = sems("raw_loaded", SLOTS)
        out_stored = sem("out_stored")
        a_freed = sems("a_freed", 2)
        a_hi_ready = sems("a_hi_ready", SLOTS)
        a_lo_ready = sems("a_lo_ready", SLOTS)
        rows_added = sem("rows_added")
        bias_masked = sem("bias_masked")
        xb_ready = sems("xb_ready", 2)
        agg_done = sems("agg_done", 2)
        xt_done = sems("xt_done", 2)
        pre_done = sems("pre_done", 2)
        node_done = sems("node_done", 2)
        rows_done = sems("rows_done", 2)
        lift_done = sems("lift_done", 2)
        msg_done = sems("msg_done", 2)
        xt_ready = sems("xt_ready", 2)
        x_term_done = sems("x_term_done", 2)
        work_ready = sems("work_ready", 2)
        feat_hi_ready = sem("feat_hi_ready")
        feat_lo_ready = sem("feat_lo_ready")
        rows_ready = sems("rows_ready", 2)
        lifted = sems("lifted", 2)
        msg_biased = sems("msg_biased", 2)
        stat_hi_ready = sems("stat_hi_ready", 2)
        stat_ready = sems("stat_ready", 2)
        y_masked = sem("y_masked")
        y_done = sems("y_done", 2)
        ln_sum = sem("ln_sum")
        ln_centered = sem("ln_centered")
        ln_squared = sem("ln_squared")
        ln_sqsum = sem("ln_sqsum")
        ln_std = sem("ln_std")
        ln_rstd = sem("ln_rstd")
        ln_scaled = sem("ln_scaled")

        def begins(u):
            return isinstance(u, int) and u == 0

        def batch(s, u):
            return u * 2 + s

        def n_agg(k, h, u):
            return u * 16 + (2 * k + h + 1)

        def n_stat(k, h, u):
            return u * 16 + (2 * k + h + 1)

        def n_residual(k, u):
            return u * 4 + (LN_OF[k] + 1)

        def n_node(k, h, u):
            return u * 8 + (2 * LN_OF[k] + h + 1)

        def n_work(k, h, u):
            return u * 16 + (2 * k + h + 1)

        def n_half(h, u):
            return u * 2 + (h + 1)

        def n_lift(k, h, u):
            return u * 4 + (2 * LIFT_OF[k] + h + 1)

        def n_msg(k, h, u):
            return u * 8 + (2 * MSG_OF[k] + h + 1)

        def n_ln(k, s, h, u):
            return u * 16 + (4 * LN_OF[k] + 2 * s + h + 1)

        def n_fill(k, s, h, u):
            return u * (2 * len(FILLS)) + (2 * FILLS.index((k, s)) + h + 1)

        def cols(h):
            return slice(h * HALF, (h + 1) * HALF)

        def per_node(a, h=None):
            if h is None:
                return a.unsqueeze(2).to_broadcast([P, CH, D])
            return a[:, h * HC:(h + 1) * HC].unsqueeze(2).to_broadcast([P, HC, D])

        def per_feature(name):
            return bias[:, BCOL[name]:BCOL[name] + D].unsqueeze(1).to_broadcast([P, CH, D])

        def stat_hi(s, k, h):
            return stat[s][:, h * HC:(h + 1) * HC, 0:D if k in NARROW_K else HID]

        def stat_lo(s, k, h):
            w = D if k in NARROW_K else HID
            return stat[s][:, h * HC:(h + 1) * HC, w:2 * w]

        def half_of(a, h):
            return a[:, h * HC:(h + 1) * HC, :]

        def node_form(a, h):
            return a[:, cols(h)].rearrange("p (c n) -> p c n", n=HID)

        block = ctx.enter_context(nc.Block())

        @block.sync
        def _(sp):
            def load_raw(s, u, first=None):
                b = batch(s, u)
                if first is None:
                    sp.wait_ge(a_lo_ready[0], b)
                for j in first or range(SLOTS):
                    if first is None:
                        sp.wait_ge(rows_added, (b - 1) * (CH - 1) + (2 * j + 1))
                        if j > 0:
                            sp.wait_ge(a_lo_ready[j], b)
                    sp.dma_start(raw[:, 2 * j:2 * j + 2, :], adj_t[b, :, 2 * j:2 * j + 2, :]).then_inc(raw_loaded[j], 16)

            def load_x(s, u, last_s=None, last_u=None):
                if last_s is not None:
                    sp.wait_ge(xb_ready[last_s], last_u * 4 + 1)
                    sp.wait_ge(stat_ready[last_s], n_stat(0, 1, last_u))
                sp.dma_start(x_in[:], x[batch(s, u)]).then_inc(x_loaded, 16)

            def load_mask(s, u):
                if not begins(u):
                    sp.wait_ge(out_stored, (batch(s, u) - 1) * 16)
                sp.dma_start(mk[s][:], mask[batch(s, u)]).then_inc(mask_loaded[s], 16)

            def store(s, u):
                sp.wait_ge(ln_scaled, n_ln(7, s, 1, u))
                sp.dma_start(out[batch(s, u)], spare[:]).then_inc(out_stored, 16)

            load_x(0, 0)
            load_raw(0, 0, first=range(0, 1))
            sp.dma_start(stage_w[:, 0:N_STAGE], weights).then_inc(w_loaded, 16)
            load_raw(0, 0, first=range(1, SLOTS - 1))
            sp.wait_ge(w_ready, 1)
            load_raw(0, 0, first=range(SLOTS - 1, SLOTS))
            sp.dma_start(bias[:], biases).then_inc(bias_loaded, 16)
            sp.dma_start(w_whole[:], whole).then_inc(whole_loaded, 16)
            load_mask(0, 0)
            load_mask(1, 0)
            load_x(1, 0, 0, 0)
            load_raw(1, 0)

            def pair(u, more):
                if more:
                    load_raw(0, u + 1)
                    load_x(0, u + 1, 1, u)
                store(0, u)
                if more:
                    load_mask(0, u + 1)
                    load_raw(1, u + 1)
                    load_x(1, u + 1, 0, u + 1)
                store(1, u)
                if more:
                    load_mask(1, u + 1)

            with sp.Fori(0, PAIRS - 1) as u:
                pair(u, True)
            pair(PAIRS - 1, False)
            sp.wait_ge(out_stored, 16 * B)

        @block.gpsimd
        def _(pool):
            def add_rows(s, u, j):
                b = batch(s, u)
                pool.wait_ge(raw_loaded[j], (b + 1) * 16)
                at = b * (CH - 1) + 2 * j
                if j == 0:
                    if not begins(u):
                        pool.wait_ge(lifted[s], u * 4)
                    nc.gpsimd.tensor_tensor(rows[s][:], raw[:, 0], raw[:, 1], ALU.add).then_inc(rows_added, 1)
                    return
                for c in range(2):
                    pool.wait_ge(rows_added, at - 1 + c)
                    nc.gpsimd.tensor_tensor(rows[s][:], rows[s][:], raw[:, 2 * j + c], ALU.add).then_inc(rows_added, 1)

            def residual0(s, u):
                if begins(u):
                    pool.wait_ge(bias_loaded, 16)
                pool.wait_ge(x_loaded, (batch(s, u) + 1) * 16)
                if not begins(u):
                    pool.wait_ge(y_done[s], u * 8)
                nc.gpsimd.tensor_tensor(xn[s][:], x_in[:], per_feature("w2"), ALU.add).then_inc(xb_ready[s], 1)

            def take_batch(s, u):
                j = SLOTS - 1
                for i in range(j):
                    add_rows(s, u, i)
                if s == 0:
                    residual0(s, u)
                if not (s == 0 and begins(u)):
                    pool.wait_ge(a_hi_ready[j], batch(s, u) + 1)
                    nc.gpsimd.tensor_tensor(a_lo[s][:, 2 * j:2 * j + 2], raw[:, 2 * j:2 * j + 2],
                                            a_hi[s][:, 2 * j:2 * j + 2].bitcast(F32), ALU.subtract).then_inc(a_lo_ready[j], 1)
                add_rows(s, u, j)
                if s == 1:
                    residual0(s, u)

            def residual(s, u, k):
                if k > 0:
                    n = u * 4 + (2 * (LN_OF[k] - 1) + s + 1)
                    for r in range(2):
                        pool.wait_ge(mask_loaded[r], (u + 1) * 16)
                    pool.wait_ge(xb_ready[1 - s], n_residual(k, u) + s)
                    nc.gpsimd.tensor_tensor(spare[:], per_node(mk[s][:]), per_feature("proj" if k == 1 else "dout"),
                                            ALU.mult).then_inc(bias_masked, 1)
                    pool.wait_ge(bias_masked, n)
                pool.wait_ge(stat_ready[s], n_stat(k + 1, 1, u))
                term = per_feature("gcn") if k == 0 else spare[:]
                nc.gpsimd.tensor_tensor(xn[s][:], xn[s][:], term, ALU.add).then_inc(xb_ready[s], 1)

            take_batch(0, 0)
            take_batch(1, 0)

            def pair(u, more):
                for k in (0, 1, 4):
                    for s in range(2):
                        residual(s, u, k)
                if more:
                    for s in range(2):
                        take_batch(s, u + 1)

            with pool.Fori(0, PAIRS - 1) as u:
                pair(u, True)
            pair(PAIRS - 1, False)

        @block.scalar
        def _(act):
            def split_adj(s, u, freed):
                b = batch(s, u)
                for j in range(SLOTS):
                    act.wait_ge(raw_loaded[j], (b + 1) * 16)
                    if freed is not None:
                        if j < SLOTS - 1:
                            act.wait_ge(a_freed[s], freed * (SLOTS - 1) + (j + 1))
                        else:
                            act.wait_ge(agg_done[s], n_agg(7, 1, freed))
                    nc.scalar.activation(a_hi[s][:, 2 * j:2 * j + 2], raw[:, 2 * j:2 * j + 2], ACT.Copy).then_inc(a_hi_ready[j], 1)

            def round_x(s, u, last):
                act.wait_ge(x_loaded, (batch(s, u) + 1) * 16)
                if last is not None:
                    act.wait_ge(agg_done[s], n_agg(7, 1, last))
                for h in range(2):
                    nc.scalar.activation(stat_hi(s, 0, h), half_of(x_in, h), ACT.Copy).then_inc(stat_hi_ready[s], 1)

            def fill(k, s, u):
                for h in range(2):
                    if k == 0:
                        act.wait_ge(x_term_done[s], n_half(h, u))
                    elif k == 1 and s == 0:
                        act.wait_ge(pre_done[1], n_half(h, u))
                    elif k == 1:
                        act.wait_ge(rows_done[0], n_half(h, u))
                    elif k == 2 and s == 0:
                        act.wait_ge(rows_done[1], n_half(h, u))
                    elif s == 1:
                        act.wait_ge(lift_done[0], n_lift(k, h, u))
                    else:
                        act.wait_ge(lift_done[1], n_lift(2, h, u))
                    if k == 1:
                        act.wait_ge(rows_added, (batch(s, u) + 1) * (CH - 1))
                        source = rows[s]
                    else:
                        act.wait_ge(agg_done[s], n_agg(k, h, u))
                        source = agg[s]
                    nc.scalar.activation(feat_hi[:, cols(h)], source[:, cols(h)], ACT.Copy).then_inc(feat_hi_ready, 1)

            def take_x_features(s, u):
                if s == 1:
                    for h in range(2):
                        act.wait_ge(pre_done[0], n_half(h, u))
                act.wait_ge(xt_done[s], u + 1)
                nc.scalar.activation(feat_hi[:], den[s][:], ACT.Copy).then_inc(xt_ready[s], 1)

            def take_aggregate(k, s, u):
                for h in range(2):
                    act.wait_ge(agg_done[s], n_agg(k, h, u))
                    nc.scalar.activation(work[s][:, cols(h)], agg[s][:, cols(h)],
                                         ACT.Copy if k == 1 else ACT.Relu).then_inc(work_ready[s], 1)

            def load_table(fn, loads):
                act.wait_ge(table_loaded, loads)
                nc.scalar.activation(idle[:], eps[:], fn).then_inc(table_loaded, 1)

            def norm(k, s, u):
                for h in range(2):
                    act.wait_ge(ln_centered, n_ln(k, s, h, u))
                    nc.scalar.activation(half_of(sq[s], h), half_of(y[s], h), ACT.Square).then_inc(ln_squared, 1)
                for h in range(2):
                    act.wait_ge(ln_sqsum, n_ln(k, s, h, u))
                    c = slice(h * HC, (h + 1) * HC)
                    nc.scalar.activation(ln_d[:, c], ln_q[:, c], ACT.Sqrt, bias=eps[:, 0:1], scale=1.0 / D).then_inc(ln_std, 1)
                if k < 7:
                    for h in range(2):
                        act.wait_ge(ln_scaled, n_ln(k, s, h, u))
                        nc.scalar.activation(stat_hi(s, k + 1, h), half_of(xn[s], h), ACT.Copy).then_inc(stat_hi_ready[s], 1)

            def finish(k, s, u):
                if k == 0:
                    load_table(ACT.Tanh, u * 4 + (2 * s + 1))
                    for h in range(2):
                        act.wait_ge(pre_done[s], n_half(h, u))
                        nc.scalar.activation(work[s][:, cols(h)], den[s][:, cols(h)], ACT.Tanh,
                                             bias=bias[:, BCOL["tanh"]:BCOL["tanh"] + 1]).then_inc(work_ready[s], 1)
                    load_table(ACT.Sqrt, u * 4 + (2 * s + 2))
                elif k in LIFT_OF:
                    fill(k, s, u)
                    for h in range(2):
                        act.wait_ge(lifted[s], n_lift(k, h, u))
                        nc.scalar.activation(work[s][:, cols(h)], work[s][:, cols(h)], ACT.Relu).then_inc(work_ready[s], 1)
                else:
                    take_aggregate(k, s, u)
                if k == 1:
                    fill(k, s, u)
                    for h in range(2):
                        act.wait_ge(rows_done[s], n_half(h, u))
                        nc.scalar.activation(rows[s][:, cols(h)], agg[s][:, cols(h)], ACT.Copy).then_inc(rows_ready[s], 1)
                if k in MSG_OF:
                    for h in range(2):
                        act.wait_ge(msg_biased[s], n_msg(k, h, u))
                        nc.scalar.activation(stat_hi(s, k + 1, h), node_form(work[s], h), ACT.Copy).then_inc(stat_hi_ready[s], 1)

            def start_stage0(s, u):
                take_x_features(s, u)
                fill(0, s, u)

            act.wait_ge(eps_set, 1)
            nc.scalar.activation(idle[:], eps[:], ACT.Tanh).then_inc(table_loaded, 1)
            round_x(0, 0, None)
            split_adj(0, 0, None)
            act.wait_ge(bias_loaded, 16)
            start_stage0(0, 0)
            round_x(1, 0, None)
            split_adj(1, 0, None)

            def pair(u, more):
                finish(0, 0, u)
                norm(0, 0, u)
                start_stage0(1, u)
                finish(0, 1, u)
                norm(0, 1, u)
                for k, s in ORDER[2:-2]:
                    finish(k, s, u)
                    if k in LN_OF:
                        norm(k, s, u)
                finish(7, 0, u)
                norm(7, 0, u)
                if more:
                    round_x(0, u + 1, u)
                    split_adj(0, u + 1, u)
                finish(7, 1, u)
                if more:
                    round_x(1, u + 1, u)
                    split_adj(1, u + 1, u)
                    start_stage0(0, u + 1)
                norm(7, 1, u)

            with act.Fori(0, PAIRS - 1) as u:
                pair(u, True)
            pair(PAIRS - 1, False)

        @block.vector
        def _(dve):
            def split_adj(s, u):
                b = batch(s, u)
                for j in range(SLOTS if s == 0 and begins(u) else SLOTS - 1):
                    dve.wait_ge(a_hi_ready[j], b + 1)
                    nc.vector.tensor_tensor(a_lo[s][:, 2 * j:2 * j + 2], raw[:, 2 * j:2 * j + 2],
                                            a_hi[s][:, 2 * j:2 * j + 2].bitcast(F32), ALU.subtract).then_inc(a_lo_ready[j], 1)

            def split_stat(s, u, k, source):
                for h in range(2):
                    dve.wait_ge(stat_hi_ready[s], n_stat(k, h, u))
                    nc.vector.tensor_tensor(stat_lo(s, k, h), source(h), stat_hi(s, k, h).bitcast(F32),
                                            ALU.subtract).then_inc(stat_ready[s], 1)

            def fill(k, s, u):
                for h in range(2):
                    dve.wait_ge(feat_hi_ready, n_fill(k, s, h, u))
                    nc.vector.tensor_tensor(feat_lo[:, cols(h)], (rows if k == 1 else agg)[s][:, cols(h)],
                                            feat_hi[:, cols(h)].bitcast(F32), ALU.subtract).then_inc(feat_lo_ready, 1)

            def add_row_bias(k, s, u):
                b = BCOL[LIFT_W[k]]
                for h in range(2):
                    if k == 2:
                        dve.wait_ge(rows_ready[s], n_half(h, u))
                    dve.wait_ge(lift_done[s], n_lift(k, h, u))
                    nc.vector.scalar_tensor_tensor(out=work[s][:, cols(h)], in0=rows[s][:, cols(h)], scalar=bias[:, b:b + 1],
                                                   in1=den[s][:, cols(h)], op0=ALU.mult, op1=ALU.add).then_inc(lifted[s], 1)

            def add_msg_bias(k, s, u):
                source = agg[s] if k in LIFT_OF else den[s]
                b = BCOL[MSG_W[k]]
                b_all = bias[:, b:b + HID].unsqueeze(1).to_broadcast([P, HC, HID])
                for h in range(2):
                    dve.wait_ge(msg_done[s], n_msg(k, h, u))
                    nc.vector.tensor_tensor(node_form(work[s], h), node_form(source, h), b_all, ALU.add).then_inc(msg_biased[s], 1)
                split_stat(s, u, k + 1, lambda h: node_form(work[s], h))

            def norm(k, s, u):
                source = [(agg if k == 0 else den)[s][:, h * HALF:h * HALF + HC * D].rearrange("p (c d) -> p c d", d=D) for h in range(2)]
                if k >= 4:
                    dve.wait_ge(mask_loaded[s], (u + 1) * 16)
                    for h in range(2):
                        dve.wait_ge(node_done[s], n_node(k, h, u))
                        nc.vector.tensor_tensor(half_of(y[s], h), source[h], per_node(mk[s], h), ALU.mult).then_inc(y_masked, 1)
                dve.wait_ge(xb_ready[s], n_residual(k, u))
                for h in range(2):
                    if k >= 4:
                        dve.wait_ge(y_masked, u * 8 + (4 * (LN_OF[k] - 2) + 2 * s + h + 2))
                        nc.vector.tensor_tensor(half_of(y[s], h), half_of(y[s], h), half_of(xn[s], h), ALU.add).then_inc(y_done[s], 1)
                    else:
                        dve.wait_ge(node_done[s], n_node(k, h, u))
                        nc.vector.tensor_tensor(half_of(y[s], h), source[h], half_of(xn[s], h), ALU.add).then_inc(y_done[s], 1)
                c = [slice(h * HC, (h + 1) * HC) for h in range(2)]
                for h in range(2):
                    dve.wait_ge(y_done[s], n_node(k, h, u))
                    nc.vector.tensor_reduce(ln_s[:, c[h]], half_of(y[s], h), AX_X, ALU.add).then_inc(ln_sum, 1)
                for h in range(2):
                    dve.wait_ge(ln_sum, n_ln(k, s, h, u))
                    nc.vector.scalar_tensor_tensor(out=half_of(y[s], h), in0=per_node(ln_s, h), scalar=-1.0 / D, in1=half_of(y[s], h),
                                                   op0=ALU.mult, op1=ALU.add).then_inc(ln_centered, 1)
                for h in range(2):
                    dve.wait_ge(ln_squared, n_ln(k, s, h, u))
                    nc.vector.tensor_reduce(ln_q[:, c[h]], half_of(sq[s], h), AX_X, ALU.add).then_inc(ln_sqsum, 1)
                if k == 7:
                    if s == 0:
                        dve.wait_ge(mask_loaded[1], (u + 1) * 16)
                    else:
                        dve.wait_ge(out_stored, batch(0, u) * 16 + 16)
                    for r in range(2):
                        dve.wait_ge(xb_ready[r], n_residual(7, u))
                for h in range(2):
                    dve.wait_ge(ln_std, n_ln(k, s, h, u))
                    nc.vector.reciprocal(ln_r[:, c[h]], ln_d[:, c[h]]).then_inc(ln_rstd, 1)
                for h in range(2):
                    dve.wait_ge(ln_rstd, n_ln(k, s, h, u))
                    nc.vector.tensor_tensor(half_of(spare if k == 7 else xn[s], h), half_of(y[s], h), per_node(ln_r, h),
                                            ALU.mult).then_inc(ln_scaled, 1)
                if k < 7:
                    split_stat(s, u, k + 1, lambda h: half_of(xn[s], h))

            def finish(k, s, u):
                if k in (1, 2, 5):
                    fill(k, s, u)
                if k in LIFT_OF:
                    add_row_bias(k, s, u)
                if k in MSG_OF:
                    add_msg_bias(k, s, u)
                if k in LN_OF:
                    norm(k, s, u)

            nc.vector.memset(eps[:], EPS).then_inc(eps_set, 1)
            nc.vector.memset(ln_s[:], 0.0).then_inc(y_masked, 1)
            dve.wait_ge(x_loaded, 16)
            split_stat(0, 0, 0, lambda h: half_of(x_in, h))
            dve.wait_ge(w_loaded, 16)
            nc.vector.tensor_copy(w_hi[:, 0:N_SPLIT], stage_w[:, 0:N_SPLIT]).then_inc(w_rounded, 1)
            dve.wait_ge(w_rounded, 1)
            nc.vector.tensor_tensor(w_lo[:, 0:N_SPLIT - N_EXACT], stage_w[:, N_EXACT:N_SPLIT],
                                    w_hi[:, N_EXACT:N_SPLIT].bitcast(F32), ALU.subtract)
            dve.wait_ge(w_product, 1)
            nc.vector.tensor_copy(w_hi[:, N_SPLIT:N_SPLIT + P], den[1][:, 0:P]).then_inc(w_rounded, 1)
            dve.wait_ge(w_rounded, 2)
            nc.vector.tensor_tensor(w_lo[:, N_SPLIT - N_EXACT:], den[1][:, 0:P], w_hi[:, N_SPLIT:N_SPLIT + P].bitcast(F32),
                                    ALU.subtract).then_inc(w_ready, 1)
            split_adj(0, 0)
            fill(0, 0, 0)
            dve.wait_ge(x_loaded, 32)
            split_stat(1, 0, 0, lambda h: half_of(x_in, h))
            split_adj(1, 0)

            def pair(u, more):
                norm(0, 0, u)
                fill(0, 1, u)
                norm(0, 1, u)
                for k, s in ORDER[2:-1]:
                    finish(k, s, u)
                if more:
                    for s in range(2):
                        split_stat(s, u + 1, 0, lambda h: half_of(x_in, h))
                        split_adj(s, u + 1)
                    fill(0, 0, u + 1)
                norm(7, 1, u)

            with dve.Fori(0, PAIRS - 1) as u:
                pair(u, True)
            pair(PAIRS - 1, False)

        @block.tensor
        def _(pe):
            def w(part, name):
                at = HI_COL[name] - (N_EXACT if part is w_lo else 0)
                return part[:, at:at + P]

            def feature_layer(target, terms, h, start=True, stop=True):
                for i, (wt, src) in enumerate(terms):
                    ins = nc.tensor.matmul(target[:, cols(h)], wt, src[:, cols(h)],
                                           start=(start and i == 0), stop=(stop and i == len(terms) - 1))
                return ins

            def split_terms(name):
                return [(w(w_hi, name), feat_hi), (w(w_hi, name), feat_lo), (w(w_lo, name), feat_hi)]

            def node_layer(target, s, name, width, h):
                at = WHOLE_COL[name]
                for i in range(HC):
                    c, out_at = h * HC + i, h * HALF + i * width
                    ins = nc.tensor.matmul(target[:, out_at:out_at + width], work[s][:, c * P:(c + 1) * P],
                                           w_whole[:, at:at + width], start=True, stop=True)
                return ins

            def first_dense(k, s, u):
                for h in range(2):
                    if k == 0:
                        pe.wait_ge(feat_lo_ready, n_fill(k, s, h, u))
                        feature_layer(den[s], split_terms("w1b"), h, start=False).then_inc(pre_done[s], 1)
                    elif k in LIFT_OF:
                        pe.wait_ge(feat_lo_ready, n_fill(k, s, h, u))
                        feature_layer(den[s], split_terms(LIFT_W[k]), h).then_inc(lift_done[s], 1)
                    elif k in MSG_OF:
                        pe.wait_ge(work_ready[s], n_work(k, h, u))
                        node_layer(den[s], s, MSG_W[k], HID, h).then_inc(msg_done[s], 1)
                    else:
                        pe.wait_ge(work_ready[s], n_work(k, h, u))
                        node_layer(den[s], s, NODE_W[k], D, h).then_inc(node_done[s], 1)

            def second_dense(k, s, u):
                for h in range(2):
                    if k == 0:
                        pe.wait_ge(work_ready[s], n_work(k, h, u))
                        node_layer(agg[s], s, "w2", D, h).then_inc(node_done[s], 1)
                    elif k == 1:
                        pe.wait_ge(feat_lo_ready, n_fill(k, s, h, u))
                        feature_layer(agg[s], [(w(w_hi, "ones"), feat_hi), (w(w_hi, "ones"), feat_lo)], h).then_inc(rows_done[s], 1)
                    elif k in LIFT_OF:
                        pe.wait_ge(work_ready[s], n_work(k, h, u))
                        node_layer(agg[s], s, MSG_W[k], HID, h).then_inc(msg_done[s], 1)

            def transpose_x(s):
                for c in range(CH):
                    ins = nc.tensor.matmul(den[s][:, c * P:(c + 1) * P], stat[s][:, c, 0:P], w(w_hi, "ident"), start=True, stop=True)
                ins.then_inc(xt_done[s], 1)

            def x_term(s, u):
                pe.wait_ge(xt_ready[s], u + 1)
                for h in range(2):
                    feature_layer(den[s], [(w(w_hi, "w1a"), feat_hi), (w(w_lo, "w1a"), feat_hi)], h, stop=False).then_inc(x_term_done[s], 1)

            def aggregate(k, s, u, start, stop):
                if k in NARROW_K:
                    terms = [(a_hi, slice(0, P)), (a_lo, slice(0, P))]
                else:
                    terms = [(a_hi, slice(0, P)), (a_hi, slice(P, 2 * P)), (a_lo, slice(0, P))]
                last = len(terms) - 1
                if k == 0:
                    steps = [(c, i, h) for c in range(CH) for i in range(len(terms)) for h in range(2)]
                else:
                    steps = [(c, i, h) for h in range(2) for c in range(CH) for i in range(len(terms))]
                for n, (c, i, h) in list(enumerate(steps))[start:stop]:
                    if n == 0 or (c == HC and i == 0 and h == 0):
                        pe.wait_ge(stat_ready[s], n_stat(k, c // HC, u))
                    if k == 2 and c == 0 and i == 0:
                        pe.wait_ge(rows_ready[s], n_half(h, u))
                    if k == 0 and c % 2 == 0 and i == 0 and h == 0:
                        pe.wait_ge(a_lo_ready[c // 2], batch(s, u) + 1)
                    src, at = terms[i]
                    ins = nc.tensor.matmul(agg[s][:, cols(h)], stat[s][:, c, at], src[s][:, c, cols(h)],
                                           start=(c == 0 and i == 0), stop=(c == CH - 1 and i == last))
                    if c == CH - 1 and i == last:
                        ins.then_inc(agg_done[s], 1)
                    elif k == 7 and h == 1 and c % 2 == 1 and i == last:
                        ins.then_inc(a_freed[s], 1)

            def stage(k, s, u, k0, s0, u0):
                aggregate(k, s, u, 0, FIRST_AT)
                first_dense(k0, s0, u0)
                if k == 0:
                    aggregate(k, s, u, FIRST_AT, XT_AT)
                    if s == 1:
                        pe.wait_ge(y_masked, u * 8 + 1)
                    transpose_x(s)
                    aggregate(k, s, u, XT_AT, SECOND_AT)
                    second_dense(k0, s0, u0)
                    aggregate(k, s, u, SECOND_AT, X_TERM_AT)
                    x_term(s, u)
                    aggregate(k, s, u, X_TERM_AT, None)
                else:
                    aggregate(k, s, u, FIRST_AT, SECOND_AT)
                    second_dense(k0, s0, u0)
                    aggregate(k, s, u, SECOND_AT, None)

            pe.wait_ge(w_loaded, 16)
            nc.tensor.matmul(den[1][:, 0:P], stage_w[:, EMBED:EMBED + P], stage_w[:, ENC0:ENC0 + P],
                             start=True, stop=True).then_inc(w_product, 1)
            pe.wait_ge(w_ready, 1)
            aggregate(0, 0, 0, 0, XT_AT)
            transpose_x(0)
            aggregate(0, 0, 0, XT_AT, X_TERM_AT)
            x_term(0, 0)
            aggregate(0, 0, 0, X_TERM_AT, None)
            pe.wait_ge(whole_loaded, 16)

            def pair(u, more):
                for (k0, s0), (k, s) in zip(ORDER, ORDER[1:]):
                    stage(k, s, u, k0, s0, u)
                if more:
                    stage(0, 0, u + 1, 7, 1, u)
                else:
                    first_dense(7, 1, u)

            with pe.Fori(0, PAIRS - 1) as u:
                pair(u, True)
            pair(PAIRS - 1, False)


def kernel(**inputs):
    import concourse.bacc as bacc
    from concourse.bass_utils import run_bass_kernel_spmd

    a = {k: np.asarray(v) for k, v in inputs.items()}

    def nodes(v):
        return np.ascontiguousarray(v.reshape(B, CH, P, -1).transpose(0, 2, 1, 3))

    def twice(v):
        return np.concatenate([v, v], axis=0)

    w1 = a["L0_gnn_W1"]
    parts = {
        "ones": np.ones((P, P), np.float32), "ident": np.eye(P, dtype=np.float32),
        "w1b": np.tile(w1[D:], (2, 2)), "w1a": np.tile(w1[:D], (2, 2)),
        "enc1": a["L2_gnn_Wl"][1], "enc2": a["L2_gnn_Wl"][2],
        "dec0": twice(a["L3_gnn_W0"]), "dec1": a["L3_gnn_W1"], "dec2": a["L3_gnn_W2"],
        "w2": np.concatenate([a["L0_gnn_W2"], np.zeros_like(a["L0_gnn_W2"])]), "gcn": twice(a["L1_gnn_weight"]),
        "proj": a["L2_gnn_W_proj"], "dout": a["L3_gnn_Wout"],
    }
    embed = a["L2_gnn_W_embed"].T
    weights = np.concatenate([parts[n] for n in EXACT + SPLIT] + [embed, embed, a["L2_gnn_Wl"][0]], axis=1)
    whole = np.concatenate([parts[n] for n in WIDE + NARROW], axis=1)
    along = [a["L2_gnn_bl"][1], a["L2_gnn_bl"][2], a["L3_gnn_b1"], a["L3_gnn_b2"],
             a["L0_gnn_b2"], a["L1_gnn_bias"], a["L2_gnn_b_proj"], a["L3_gnn_bout"]]
    down = [np.tile(a["L0_gnn_b1"], 2), a["L2_gnn_bl"][0], a["L3_gnn_b0"]]
    biases = np.concatenate([np.tile(np.concatenate(along), (P, 1)), np.stack(down, axis=1)], axis=1)
    arrays = {
        "x": nodes(a["x"]),
        "adj_t": nodes(a["adj"].transpose(0, 2, 1)),
        "mask": np.ascontiguousarray(a["nodemask"].reshape(B, CH, P).transpose(0, 2, 1)),
        "weights": np.ascontiguousarray(weights),
        "whole": np.ascontiguousarray(whole),
        "biases": np.ascontiguousarray(biases),
    }

    nc = bacc.Bacc("TRN2", target_bir_lowering=False, num_devices=1, dynamic_dma_scratch_size=1024)
    aps = {n: nc.dram_tensor(n, v.shape, mybir.dt.from_np(v.dtype), kind="ExternalInput").ap() for n, v in arrays.items()}
    out = nc.dram_tensor("out", (B, P, CH, D), F32, kind="ExternalOutput").ap()
    graph_networks(nc, aps["x"], aps["adj_t"], aps["mask"], aps["weights"], aps["whole"], aps["biases"], out)
    r = run_bass_kernel_spmd(nc, [arrays], core_ids=[0])
    return np.ascontiguousarray(r.results[0]["out"].transpose(0, 2, 1, 3)).reshape(B, N, D)
```

```python
from contextlib import ExitStack

import numpy as np

import concourse.bass as bass
from concourse import mybir


P = 128
B, N, D, HID = 8, 1024, 64, 128
CH = N // P
HALF = N // 2
HC = CH // 2
PAIRS = B // 2
SLOTS = CH // 2
EPS = 1e-5

F32 = mybir.dt.float32
F32R = mybir.dt.float32r
ALU = mybir.AluOpType
ACT = mybir.ActivationFunctionType
AX_X = mybir.AxisListType.X

EXACT = ["ones", "ident"]
SPLIT = ["w1b", "w1a", "dec0"]
WIDE = ["enc1", "enc2", "dec1", "dec2"]
NARROW = ["w2", "gcn", "proj", "dout"]
N_EXACT = len(EXACT) * P
N_SPLIT = N_EXACT + len(SPLIT) * P
N_WHOLE = len(WIDE) * P + len(NARROW) * D
HI_COL = {n: i * P for i, n in enumerate(EXACT + SPLIT + ["enc0"])}
WHOLE_COL = {n: i * P for i, n in enumerate(WIDE)}
WHOLE_COL |= {n: len(WIDE) * P + i * D for i, n in enumerate(NARROW)}
EMBED, ENC0, N_STAGE = N_SPLIT, N_SPLIT + P, N_SPLIT + 2 * P
BCOL = {"enc1": 0, "enc2": 128, "dec1": 256, "dec2": 384, "w2": 512, "gcn": 576, "proj": 640, "dout": 704,
        "tanh": 768, "enc0": 769, "dec0": 770}
N_BIAS = 771

DENSE_AT = {(k, s): (5, 22) for k in range(8) for s in range(2)}
DENSE_AT |= {(0, 0): (8, 18), (0, 1): (8, 15), (7, 1): (10, 10), (1, 0): (5, 16), (1, 1): (5, 16)}
XT_AT, X_TERM_AT = (12, 14), 28

LN_OF = {0: 0, 1: 1, 4: 2, 7: 3}
LIFT_OF = {2: 0, 5: 1}
MSG_OF = {2: 0, 3: 1, 5: 2, 6: 3}
LIFT_W = {2: "enc0", 5: "dec0"}
MSG_W = {2: "enc1", 3: "enc2", 5: "dec1", 6: "dec2"}
NODE_W = {1: "gcn", 4: "proj", 7: "dout"}
NARROW_K = (0, 1, 2, 5)
ORDER = [(k, s) for k in range(8) for s in range(2)]
FILLS = [(k, s) for k in (0, 1, 2, 5) for s in range(2)]


def graph_networks(nc: bass.Bass, x, adj_t, mask, weights, whole, biases, out):
    with ExitStack() as ctx:
        def sb(name, shape, dt=F32):
            return ctx.enter_context(nc.sbuf_tensor(name, shape, dt))

        def sem(name):
            return ctx.enter_context(nc.semaphore(name))

        def sems(name, n):
            return [sem(f"{name}{i}") for i in range(n)]

        a_hi = [sb(f"a_hi{s}", [P, CH, N], F32R) for s in range(2)]
        a_lo = [sb(f"a_lo{s}", [P, CH, N], F32R) for s in range(2)]
        raw = sb("raw", [P, CH, N])
        stat = [sb(f"stat{s}", [P, CH, 2 * HID], F32R) for s in range(2)]
        feat_hi = sb("feat_hi", [P, N], F32R)
        feat_lo = sb("feat_lo", [P, N], F32R)
        rows = [sb(f"rows{s}", [P, N]) for s in range(2)]
        work = [sb(f"work{s}", [P, N]) for s in range(2)]
        xn = [sb(f"xn{s}", [P, CH, D]) for s in range(2)]
        x_in = sb("x_in", [P, CH, D])
        spare = sb("spare", [P, CH, D])
        mk = [sb(f"mk{s}", [P, CH]) for s in range(2)]
        w_hi = sb("w_hi", [P, N_SPLIT + P], F32R)
        w_lo = sb("w_lo", [P, N_SPLIT + P - N_EXACT], F32R)
        w_whole = sb("w_whole", [P, N_WHOLE])
        bias = sb("bias", [P, N_BIAS])
        ln_s = [sb(f"ln_s{s}", [P, CH]) for s in range(2)]
        ln_q = [sb(f"ln_q{s}", [P, CH]) for s in range(2)]
        ln_d = [sb(f"ln_d{s}", [P, CH]) for s in range(2)]
        idle = sb("idle", [P, 1])
        ln_r = [sb(f"ln_r{s}", [P, CH]) for s in range(2)]
        eps = sb("eps", [P, 1])
        eps_set = sem("eps_set")
        table_loaded = sem("table_loaded")
        stage_w = raw[:, CH - 2:CH, :].rearrange("p c n -> p (c n)")
        y = [work[s][:, 0:HALF].rearrange("p (c d) -> p c d", d=D) for s in range(2)]
        sq = [work[s][:, HALF:N].rearrange("p (c d) -> p c d", d=D) for s in range(2)]

        agg = [ctx.enter_context(nc.psum_tensor(f"agg{s}", [P, N], F32)) for s in range(2)]
        den = [ctx.enter_context(nc.psum_tensor(f"den{s}", [P, N], F32)) for s in range(2)]

        w_loaded = sem("w_loaded")
        w_rounded = sem("w_rounded")
        w_product = sem("w_product")
        w_ready = sem("w_ready")
        whole_loaded = sem("whole_loaded")
        bias_loaded = sem("bias_loaded")
        x_loaded = sem("x_loaded")
        mask_loaded = sems("mask_loaded", 2)
        raw_loaded = sems("raw_loaded", SLOTS)
        out_stored = sem("out_stored")
        a_freed = sems("a_freed", 2)
        a_hi_ready = sems("a_hi_ready", SLOTS)
        a_lo_ready = sems("a_lo_ready", SLOTS)
        rows_added = sem("rows_added")
        bias_masked = sem("bias_masked")
        xb_ready = sems("xb_ready", 2)
        agg_done = sems("agg_done", 2)
        xt_done = sems("xt_done", 2)
        pre_done = sems("pre_done", 2)
        node_done = sems("node_done", 2)
        rows_done = sems("rows_done", 2)
        lift_done = sems("lift_done", 2)
        msg_done = sems("msg_done", 2)
        xt_ready = sems("xt_ready", 2)
        x_term_done = sems("x_term_done", 2)
        work_ready = sems("work_ready", 2)
        feat_hi_ready = sem("feat_hi_ready")
        feat_lo_ready = sem("feat_lo_ready")
        rows_ready = sems("rows_ready", 2)
        lifted = sems("lifted", 2)
        msg_biased = sems("msg_biased", 2)
        stat_hi_ready = sems("stat_hi_ready", 2)
        stat_ready = sems("stat_ready", 2)
        y_masked = sem("y_masked")
        y_done = sems("y_done", 2)
        ln_sum = sems("ln_sum", 2)
        ln_centered = sems("ln_centered", 2)
        ln_squared = sems("ln_squared", 2)
        ln_sqsum = sems("ln_sqsum", 2)
        ln_std = sems("ln_std", 2)
        ln_rstd = sems("ln_rstd", 2)
        ln_scaled = sems("ln_scaled", 2)

        def begins(u):
            return isinstance(u, int) and u == 0

        def batch(s, u):
            return u * 2 + s

        def n_agg(k, h, u):
            return u * 16 + (2 * k + h + 1)

        def n_stat(k, h, u):
            return u * 16 + (2 * k + h + 1)

        def n_residual(k, u):
            return u * 4 + (LN_OF[k] + 1)

        def n_node(k, h, u):
            return u * 8 + (2 * LN_OF[k] + h + 1)

        def n_work(k, h, u):
            return u * 16 + (2 * k + h + 1)

        def n_half(h, u):
            return u * 2 + (h + 1)

        def n_lift(k, h, u):
            return u * 4 + (2 * LIFT_OF[k] + h + 1)

        def n_msg(k, h, u):
            return u * 8 + (2 * MSG_OF[k] + h + 1)


        def n_fill(k, s, h, u):
            return u * (2 * len(FILLS)) + (2 * FILLS.index((k, s)) + h + 1)

        def cols(h):
            return slice(h * HALF, (h + 1) * HALF)

        def per_node(a, h=None):
            if h is None:
                return a.unsqueeze(2).to_broadcast([P, CH, D])
            return a[:, h * HC:(h + 1) * HC].unsqueeze(2).to_broadcast([P, HC, D])

        def per_feature(name):
            return bias[:, BCOL[name]:BCOL[name] + D].unsqueeze(1).to_broadcast([P, CH, D])

        def stat_hi(s, k, h):
            return stat[s][:, h * HC:(h + 1) * HC, 0:D if k in NARROW_K else HID]

        def stat_lo(s, k, h):
            w = D if k in NARROW_K else HID
            return stat[s][:, h * HC:(h + 1) * HC, w:2 * w]

        def chunks(h):
            return slice(h * HC, (h + 1) * HC)

        def half_of(a, h):
            return a[:, h * HC:(h + 1) * HC, :]

        def node_form(a, h):
            return a[:, cols(h)].rearrange("p (c n) -> p c n", n=HID)

        def first_x(s, u):
            return xn[1] if s == 1 and begins(u) else x_in

        block = ctx.enter_context(nc.Block())

        @block.sync
        def _(sp):
            def load_raw(s, u, first=None, slots=range(SLOTS)):
                b = batch(s, u)
                if first is None and slots[0] == 0:
                    sp.wait_ge(a_lo_ready[0], b)
                for j in first or slots:
                    if first is None:
                        sp.wait_ge(rows_added, (b - 1) * (CH - 1) + (2 * j + 1))
                        if j > 0:
                            sp.wait_ge(a_lo_ready[j], b)
                    sp.dma_start(raw[:, 2 * j:2 * j + 2, :], adj_t[b, :, 2 * j:2 * j + 2, :]).then_inc(raw_loaded[j], 16)

            def load_x(s, u, last_s=None, last_u=None):
                if last_s is not None:
                    sp.wait_ge(xb_ready[last_s], last_u * 4 + 1)
                    sp.wait_ge(stat_ready[last_s], n_stat(0, 1, last_u))
                sp.dma_start(first_x(s, u)[:], x[batch(s, u)]).then_inc(x_loaded, 16)

            def load_mask(s, u):
                if not begins(u):
                    sp.wait_ge(out_stored, (batch(s, u) - 1) * 16)
                sp.dma_start(mk[s][:], mask[batch(s, u)]).then_inc(mask_loaded[s], 16)

            def store(s, u):
                sp.wait_ge(ln_scaled[s], n_node(7, 1, u))
                sp.dma_start(out[batch(s, u)], spare[:]).then_inc(out_stored, 16)

            load_x(0, 0)
            load_raw(0, 0, first=range(0, 1))
            sp.dma_start(stage_w[:, 0:N_STAGE], weights).then_inc(w_loaded, 16)
            load_raw(0, 0, first=range(1, SLOTS - 1))
            sp.wait_ge(w_ready, 1)
            load_raw(0, 0, first=range(SLOTS - 1, SLOTS))
            load_x(1, 0)
            load_raw(1, 0, slots=range(0, 1))
            sp.dma_start(bias[:], biases).then_inc(bias_loaded, 16)
            sp.dma_start(w_whole[:], whole).then_inc(whole_loaded, 16)
            load_raw(1, 0, slots=range(1, SLOTS))
            load_mask(0, 0)
            load_mask(1, 0)

            def pair(u, more):
                if more:
                    load_raw(0, u + 1)
                    load_x(0, u + 1, 1, u)
                    load_raw(1, u + 1, slots=range(0, 2))
                store(0, u)
                if more:
                    load_x(1, u + 1, 0, u + 1)
                    load_raw(1, u + 1, slots=range(2, SLOTS))
                    load_mask(0, u + 1)
                store(1, u)
                if more:
                    load_mask(1, u + 1)

            with sp.Fori(0, PAIRS - 1) as u:
                pair(u, True)
            pair(PAIRS - 1, False)
            sp.wait_ge(out_stored, 16 * B)

        @block.gpsimd
        def _(pool):
            def add_rows(s, u, j):
                b = batch(s, u)
                pool.wait_ge(raw_loaded[j], (b + 1) * 16)
                at = b * (CH - 1) + 2 * j
                if j == 0:
                    if not begins(u):
                        pool.wait_ge(lifted[s], u * 4)
                    nc.gpsimd.tensor_tensor(rows[s][:], raw[:, 0], raw[:, 1], ALU.add).then_inc(rows_added, 1)
                    return
                for c in range(2):
                    pool.wait_ge(rows_added, at - 1 + c)
                    nc.gpsimd.tensor_tensor(rows[s][:], rows[s][:], raw[:, 2 * j + c], ALU.add).then_inc(rows_added, 1)

            def residual0(s, u):
                if begins(u):
                    pool.wait_ge(bias_loaded, 16)
                pool.wait_ge(x_loaded, (batch(s, u) + 1) * 16)
                if not begins(u):
                    pool.wait_ge(y_done[s], u * 8)
                elif s == 1:
                    pool.wait_ge(stat_ready[1], n_stat(0, 1, 0))
                nc.gpsimd.tensor_tensor(xn[s][:], first_x(s, u)[:], per_feature("w2"), ALU.add).then_inc(xb_ready[s], 1)

            def take_batch(s, u):
                j = SLOTS - 1
                if s == 0:
                    for i in range(SLOTS):
                        add_rows(s, u, i)
                if not begins(u):
                    pool.wait_ge(a_hi_ready[j], batch(s, u) + 1)
                    nc.gpsimd.tensor_tensor(a_lo[s][:, 2 * j:2 * j + 2], raw[:, 2 * j:2 * j + 2],
                                            a_hi[s][:, 2 * j:2 * j + 2].bitcast(F32), ALU.subtract).then_inc(a_lo_ready[j], 1)
                residual0(s, u)
                if s == 1:
                    for i in range(SLOTS):
                        add_rows(s, u, i)

            def residual(s, u, k):
                if k > 0:
                    n = u * 4 + (2 * (LN_OF[k] - 1) + s + 1)
                    for r in range(2):
                        pool.wait_ge(mask_loaded[r], (u + 1) * 16)
                    pool.wait_ge(xb_ready[1 - s], n_residual(k, u) + s)
                    nc.gpsimd.tensor_tensor(spare[:], per_node(mk[s][:]), per_feature("proj" if k == 1 else "dout"),
                                            ALU.mult).then_inc(bias_masked, 1)
                    pool.wait_ge(bias_masked, n)
                pool.wait_ge(stat_ready[s], n_stat(k + 1, 1, u))
                term = per_feature("gcn") if k == 0 else spare[:]
                nc.gpsimd.tensor_tensor(xn[s][:], xn[s][:], term, ALU.add).then_inc(xb_ready[s], 1)

            take_batch(0, 0)
            take_batch(1, 0)

            def pair(u, more):
                for k in (0, 1, 4):
                    for s in range(2):
                        residual(s, u, k)
                if more:
                    for s in range(2):
                        take_batch(s, u + 1)

            with pool.Fori(0, PAIRS - 1) as u:
                pair(u, True)
            pair(PAIRS - 1, False)

        @block.scalar
        def _(act):
            def split_adj(s, u, freed, slots=range(SLOTS)):
                b = batch(s, u)
                for j in slots:
                    act.wait_ge(raw_loaded[j], (b + 1) * 16)
                    if freed is not None:
                        if j < SLOTS - 1:
                            act.wait_ge(a_freed[s], freed * (SLOTS - 1) + (j + 1))
                        else:
                            act.wait_ge(agg_done[s], n_agg(7, 1, freed))
                    nc.scalar.activation(a_hi[s][:, 2 * j:2 * j + 2], raw[:, 2 * j:2 * j + 2], ACT.Copy).then_inc(a_hi_ready[j], 1)

            def round_x(s, u, last):
                act.wait_ge(x_loaded, (batch(s, u) + 1) * 16)
                if last is not None:
                    act.wait_ge(agg_done[s], n_agg(7, 1, last))
                for h in range(2):
                    nc.scalar.activation(stat_hi(s, 0, h), half_of(first_x(s, u), h), ACT.Copy).then_inc(stat_hi_ready[s], 1)

            def fill(k, s, u):
                for h in range(2):
                    if k == 0:
                        act.wait_ge(x_term_done[s], n_half(h, u))
                    elif k == 1 and s == 0:
                        act.wait_ge(pre_done[1], n_half(h, u))
                    elif k == 1:
                        act.wait_ge(rows_done[0], n_half(h, u))
                    elif k == 2 and s == 0:
                        act.wait_ge(rows_done[1], n_half(h, u))
                    elif s == 1:
                        act.wait_ge(lift_done[0], n_lift(k, h, u))
                    else:
                        act.wait_ge(lift_done[1], n_lift(2, h, u))
                    if k == 1:
                        act.wait_ge(rows_added, (batch(s, u) + 1) * (CH - 1))
                        source = rows[s]
                    else:
                        act.wait_ge(agg_done[s], n_agg(k, h, u))
                        source = agg[s]
                    nc.scalar.activation(feat_hi[:, cols(h)], source[:, cols(h)], ACT.Copy).then_inc(feat_hi_ready, 1)

            def take_x_features(s, u):
                if s == 1:
                    for h in range(2):
                        act.wait_ge(pre_done[0], n_half(h, u))
                act.wait_ge(xt_done[s], u + 1)
                nc.scalar.activation(feat_hi[:], den[s][:], ACT.Copy).then_inc(xt_ready[s], 1)

            def take_aggregate(k, s, u):
                for h in range(2):
                    act.wait_ge(agg_done[s], n_agg(k, h, u))
                    nc.scalar.activation(work[s][:, cols(h)], agg[s][:, cols(h)],
                                         ACT.Copy if k == 1 else ACT.Relu).then_inc(work_ready[s], 1)

            def load_table(fn, loads):
                act.wait_ge(table_loaded, loads)
                nc.scalar.activation(idle[:], eps[:], fn).then_inc(table_loaded, 1)

            def norm_squares(k, s, u):
                for h in range(2):
                    act.wait_ge(ln_centered[s], n_node(k, h, u))
                    nc.scalar.activation(half_of(sq[s], h), half_of(y[s], h), ACT.Square).then_inc(ln_squared[s], 1)

            def norm_scale(k, s, u):
                for h in range(2):
                    act.wait_ge(ln_sqsum[s], n_node(k, h, u))
                    c = slice(h * HC, (h + 1) * HC)
                    nc.scalar.activation(ln_d[s][:, c], ln_q[s][:, c], ACT.Sqrt, bias=eps[:, 0:1], scale=1.0 / D).then_inc(ln_std[s], 1)
                if k < 7:
                    for h in range(2):
                        act.wait_ge(ln_scaled[s], n_node(k, h, u))
                        nc.scalar.activation(stat_hi(s, k + 1, h), half_of(xn[s], h), ACT.Copy).then_inc(stat_hi_ready[s], 1)

            def norm(k, s, u):
                norm_squares(k, s, u)
                norm_scale(k, s, u)

            def finish(k, s, u):
                if k == 0:
                    load_table(ACT.Tanh, u * 4 + (2 * s + 1))
                    for h in range(2):
                        act.wait_ge(pre_done[s], n_half(h, u))
                        nc.scalar.activation(work[s][:, cols(h)], den[s][:, cols(h)], ACT.Tanh,
                                             bias=bias[:, BCOL["tanh"]:BCOL["tanh"] + 1]).then_inc(work_ready[s], 1)
                    load_table(ACT.Sqrt, u * 4 + (2 * s + 2))
                elif k in LIFT_OF:
                    fill(k, s, u)
                    for h in range(2):
                        act.wait_ge(lifted[s], n_lift(k, h, u))
                        nc.scalar.activation(work[s][:, cols(h)], work[s][:, cols(h)], ACT.Relu).then_inc(work_ready[s], 1)
                else:
                    take_aggregate(k, s, u)
                if k == 1:
                    fill(k, s, u)
                if k in MSG_OF:
                    for h in range(2):
                        act.wait_ge(msg_biased[s], n_msg(k, h, u))
                        nc.scalar.activation(stat_hi(s, k + 1, h), node_form(work[s], h), ACT.Copy).then_inc(stat_hi_ready[s], 1)

            def take_rows(s, u):
                for h in range(2):
                    act.wait_ge(rows_done[s], n_half(h, u))
                    nc.scalar.activation(rows[s][:, cols(h)], agg[s][:, cols(h)], ACT.Copy).then_inc(rows_ready[s], 1)

            act.wait_ge(eps_set, 1)
            nc.scalar.activation(idle[:], eps[:], ACT.Tanh).then_inc(table_loaded, 1)
            round_x(0, 0, None)
            split_adj(0, 0, None)
            take_x_features(0, 0)
            round_x(1, 0, None)
            split_adj(1, 0, None, range(0, 1))
            fill(0, 0, 0)
            split_adj(1, 0, None, range(1, 2))
            act.wait_ge(bias_loaded, 16)
            finish(0, 0, 0)
            split_adj(1, 0, None, range(2, SLOTS))
            take_x_features(1, 0)
            norm(0, 0, 0)

            def pair(u, more):
                fill(0, 1, u)
                finish(0, 1, u)
                norm(0, 1, u)
                for k, s in ORDER[2:-2]:
                    finish(k, s, u)
                    if k in LN_OF:
                        norm(k, s, u)
                    if k == 1:
                        take_rows(s, u)
                finish(7, 0, u)
                if more:
                    split_adj(0, u + 1, u)
                    round_x(0, u + 1, u)
                norm(7, 0, u)
                finish(7, 1, u)
                if more:
                    split_adj(1, u + 1, u, range(0, 1))
                    round_x(1, u + 1, u)
                    take_x_features(0, u + 1)
                    split_adj(1, u + 1, u, range(1, 2))
                    fill(0, 0, u + 1)
                    split_adj(1, u + 1, u, range(2, SLOTS))
                    finish(0, 0, u + 1)
                    take_x_features(1, u + 1)
                    norm_squares(7, 1, u)
                    norm(0, 0, u + 1)
                    norm_scale(7, 1, u)
                else:
                    norm(7, 1, u)

            with act.Fori(0, PAIRS - 1) as u:
                pair(u, True)
            pair(PAIRS - 1, False)

        @block.vector
        def _(dve):
            def split_adj(s, u, slots=range(SLOTS - 1)):
                b = batch(s, u)
                for j in slots:
                    dve.wait_ge(a_hi_ready[j], b + 1)
                    nc.vector.tensor_tensor(a_lo[s][:, 2 * j:2 * j + 2], raw[:, 2 * j:2 * j + 2],
                                            a_hi[s][:, 2 * j:2 * j + 2].bitcast(F32), ALU.subtract).then_inc(a_lo_ready[j], 1)

            def split_stat(s, u, k, source):
                for h in range(2):
                    dve.wait_ge(stat_hi_ready[s], n_stat(k, h, u))
                    nc.vector.tensor_tensor(stat_lo(s, k, h), source(h), stat_hi(s, k, h).bitcast(F32),
                                            ALU.subtract).then_inc(stat_ready[s], 1)

            def fill(k, s, u):
                for h in range(2):
                    dve.wait_ge(feat_hi_ready, n_fill(k, s, h, u))
                    nc.vector.tensor_tensor(feat_lo[:, cols(h)], (rows if k == 1 else agg)[s][:, cols(h)],
                                            feat_hi[:, cols(h)].bitcast(F32), ALU.subtract).then_inc(feat_lo_ready, 1)

            def add_row_bias(k, s, u):
                b = BCOL[LIFT_W[k]]
                for h in range(2):
                    if k == 2:
                        dve.wait_ge(rows_ready[s], n_half(h, u))
                    dve.wait_ge(lift_done[s], n_lift(k, h, u))
                    nc.vector.scalar_tensor_tensor(out=work[s][:, cols(h)], in0=rows[s][:, cols(h)], scalar=bias[:, b:b + 1],
                                                   in1=den[s][:, cols(h)], op0=ALU.mult, op1=ALU.add).then_inc(lifted[s], 1)

            def add_msg_bias(k, s, u):
                source = agg[s] if k in LIFT_OF else den[s]
                b = BCOL[MSG_W[k]]
                b_all = bias[:, b:b + HID].unsqueeze(1).to_broadcast([P, HC, HID])
                for h in range(2):
                    dve.wait_ge(msg_done[s], n_msg(k, h, u))
                    nc.vector.tensor_tensor(node_form(work[s], h), node_form(source, h), b_all, ALU.add).then_inc(msg_biased[s], 1)
                split_stat(s, u, k + 1, lambda h: node_form(work[s], h))

            def norm_source(k, s):
                return [(agg if k == 0 else den)[s][:, h * HALF:h * HALF + HC * D].rearrange("p (c d) -> p c d", d=D) for h in range(2)]

            def mask_source(k, s, u):
                source = norm_source(k, s)
                dve.wait_ge(mask_loaded[s], (u + 1) * 16)
                for h in range(2):
                    dve.wait_ge(node_done[s], n_node(k, h, u))
                    nc.vector.tensor_tensor(half_of(y[s], h), source[h], per_node(mk[s], h), ALU.mult).then_inc(y_masked, 1)

            def norm_center(k, s, u):
                source = norm_source(k, s)
                dve.wait_ge(xb_ready[s], n_residual(k, u))
                for h in range(2):
                    if k >= 4:
                        dve.wait_ge(y_masked, u * 8 + (4 * (LN_OF[k] - 2) + 2 * s + h + 2))
                        nc.vector.tensor_tensor(half_of(y[s], h), half_of(y[s], h), half_of(xn[s], h), ALU.add).then_inc(y_done[s], 1)
                    else:
                        dve.wait_ge(node_done[s], n_node(k, h, u))
                        nc.vector.tensor_tensor(half_of(y[s], h), source[h], half_of(xn[s], h), ALU.add).then_inc(y_done[s], 1)
                for h in range(2):
                    dve.wait_ge(y_done[s], n_node(k, h, u))
                    nc.vector.tensor_reduce(ln_s[s][:, chunks(h)], half_of(y[s], h), AX_X, ALU.add).then_inc(ln_sum[s], 1)
                for h in range(2):
                    dve.wait_ge(ln_sum[s], n_node(k, h, u))
                    nc.vector.scalar_tensor_tensor(out=half_of(y[s], h), in0=per_node(ln_s[s], h), scalar=-1.0 / D, in1=half_of(y[s], h),
                                                   op0=ALU.mult, op1=ALU.add).then_inc(ln_centered[s], 1)

            def norm_scale(k, s, u):
                for h in range(2):
                    dve.wait_ge(ln_squared[s], n_node(k, h, u))
                    nc.vector.tensor_reduce(ln_q[s][:, chunks(h)], half_of(sq[s], h), AX_X, ALU.add).then_inc(ln_sqsum[s], 1)
                if k == 7:
                    if s == 0:
                        dve.wait_ge(mask_loaded[1], (u + 1) * 16)
                    else:
                        dve.wait_ge(out_stored, batch(0, u) * 16 + 16)
                    for r in range(2):
                        dve.wait_ge(xb_ready[r], n_residual(7, u))
                for h in range(2):
                    dve.wait_ge(ln_std[s], n_node(k, h, u))
                    nc.vector.reciprocal(ln_r[s][:, chunks(h)], ln_d[s][:, chunks(h)]).then_inc(ln_rstd[s], 1)
                for h in range(2):
                    dve.wait_ge(ln_rstd[s], n_node(k, h, u))
                    nc.vector.tensor_tensor(half_of(spare if k == 7 else xn[s], h), half_of(y[s], h), per_node(ln_r[s], h),
                                            ALU.mult).then_inc(ln_scaled[s], 1)
                if k < 7:
                    split_stat(s, u, k + 1, lambda h: half_of(xn[s], h))

            def norm(k, s, u):
                if k >= 4:
                    mask_source(k, s, u)
                norm_center(k, s, u)
                norm_scale(k, s, u)

            def finish(k, s, u):
                if k in (1, 2, 5):
                    fill(k, s, u)
                if k in LIFT_OF:
                    add_row_bias(k, s, u)
                if k in MSG_OF:
                    add_msg_bias(k, s, u)
                if k in LN_OF:
                    norm(k, s, u)

            nc.vector.memset(eps[:], EPS).then_inc(eps_set, 1)
            nc.vector.memset(ln_s[0][:], 0.0).then_inc(y_masked, 1)
            dve.wait_ge(x_loaded, 16)
            split_stat(0, 0, 0, lambda h: half_of(first_x(0, 0), h))
            dve.wait_ge(w_loaded, 16)
            nc.vector.tensor_copy(w_hi[:, 0:N_SPLIT], stage_w[:, 0:N_SPLIT]).then_inc(w_rounded, 1)
            dve.wait_ge(w_rounded, 1)
            nc.vector.tensor_tensor(w_lo[:, 0:N_SPLIT - N_EXACT], stage_w[:, N_EXACT:N_SPLIT],
                                    w_hi[:, N_EXACT:N_SPLIT].bitcast(F32), ALU.subtract)
            dve.wait_ge(w_product, 1)
            nc.vector.tensor_copy(w_hi[:, N_SPLIT:N_SPLIT + P], den[1][:, 0:P]).then_inc(w_rounded, 1)
            dve.wait_ge(w_rounded, 2)
            nc.vector.tensor_tensor(w_lo[:, N_SPLIT - N_EXACT:], den[1][:, 0:P], w_hi[:, N_SPLIT:N_SPLIT + P].bitcast(F32),
                                    ALU.subtract).then_inc(w_ready, 1)
            split_adj(0, 0, range(SLOTS))
            dve.wait_ge(x_loaded, 32)
            split_stat(1, 0, 0, lambda h: half_of(first_x(1, 0), h))
            split_adj(1, 0, range(0, 1))
            fill(0, 0, 0)
            split_adj(1, 0, range(1, SLOTS))
            norm(0, 0, 0)

            def pair(u, more):
                fill(0, 1, u)
                norm(0, 1, u)
                for k, s in ORDER[2:-2]:
                    finish(k, s, u)
                if more:
                    split_adj(0, u + 1)
                    split_stat(0, u + 1, 0, lambda h: half_of(x_in, h))
                norm(7, 0, u)
                if more:
                    split_adj(1, u + 1, range(0, 1))
                    split_stat(1, u + 1, 0, lambda h: half_of(x_in, h))
                    split_adj(1, u + 1, range(1, 2))
                    fill(0, 0, u + 1)
                    mask_source(7, 1, u)
                    split_adj(1, u + 1, range(2, SLOTS - 1))
                    norm_center(7, 1, u)
                    norm(0, 0, u + 1)
                    norm_scale(7, 1, u)
                else:
                    norm(7, 1, u)

            with dve.Fori(0, PAIRS - 1) as u:
                pair(u, True)
            pair(PAIRS - 1, False)

        @block.tensor
        def _(pe):
            def w(part, name):
                at = HI_COL[name] - (N_EXACT if part is w_lo else 0)
                return part[:, at:at + P]

            def feature_layer(target, terms, h, start=True, stop=True):
                for i, (wt, src) in enumerate(terms):
                    ins = nc.tensor.matmul(target[:, cols(h)], wt, src[:, cols(h)],
                                           start=(start and i == 0), stop=(stop and i == len(terms) - 1))
                return ins

            def split_terms(name):
                return [(w(w_hi, name), feat_hi), (w(w_hi, name), feat_lo), (w(w_lo, name), feat_hi)]

            def node_layer(target, s, name, width, h):
                at = WHOLE_COL[name]
                for i in range(HC):
                    c, out_at = h * HC + i, h * HALF + i * width
                    ins = nc.tensor.matmul(target[:, out_at:out_at + width], work[s][:, c * P:(c + 1) * P],
                                           w_whole[:, at:at + width], start=True, stop=True)
                return ins

            def first_dense(k, s, u):
                for h in range(2):
                    if k == 0:
                        pe.wait_ge(feat_lo_ready, n_fill(k, s, h, u))
                        feature_layer(den[s], split_terms("w1b"), h, start=False).then_inc(pre_done[s], 1)
                    elif k in LIFT_OF:
                        pe.wait_ge(feat_lo_ready, n_fill(k, s, h, u))
                        feature_layer(den[s], split_terms(LIFT_W[k]), h).then_inc(lift_done[s], 1)
                    elif k in MSG_OF:
                        pe.wait_ge(work_ready[s], n_work(k, h, u))
                        node_layer(den[s], s, MSG_W[k], HID, h).then_inc(msg_done[s], 1)
                    else:
                        pe.wait_ge(work_ready[s], n_work(k, h, u))
                        node_layer(den[s], s, NODE_W[k], D, h).then_inc(node_done[s], 1)

            def second_dense(k, s, u):
                for h in range(2):
                    if k == 0:
                        pe.wait_ge(work_ready[s], n_work(k, h, u))
                        node_layer(agg[s], s, "w2", D, h).then_inc(node_done[s], 1)
                    elif k == 1:
                        pe.wait_ge(feat_lo_ready, n_fill(k, s, h, u))
                        feature_layer(agg[s], [(w(w_hi, "ones"), feat_hi), (w(w_hi, "ones"), feat_lo)], h).then_inc(rows_done[s], 1)
                    elif k in LIFT_OF:
                        pe.wait_ge(work_ready[s], n_work(k, h, u))
                        node_layer(agg[s], s, MSG_W[k], HID, h).then_inc(msg_done[s], 1)

            def transpose_x(s, u):
                pe.wait_ge(stat_ready[s], n_stat(0, 1, u))
                if s == 1:
                    pe.wait_ge(y_masked, u * 8 + 1)
                elif not begins(u):
                    pe.wait_ge(y_masked, u * 8 - 1)
                for c in range(CH):
                    ins = nc.tensor.matmul(den[s][:, c * P:(c + 1) * P], stat[s][:, c, 0:P], w(w_hi, "ident"), start=True, stop=True)
                ins.then_inc(xt_done[s], 1)

            def x_term(s, u):
                pe.wait_ge(xt_ready[s], u + 1)
                for h in range(2):
                    feature_layer(den[s], [(w(w_hi, "w1a"), feat_hi), (w(w_lo, "w1a"), feat_hi)], h, stop=False).then_inc(x_term_done[s], 1)

            def aggregate(k, s, u, start, stop):
                if k in NARROW_K:
                    terms = [(a_hi, slice(0, P)), (a_lo, slice(0, P))]
                else:
                    terms = [(a_hi, slice(0, P)), (a_hi, slice(P, 2 * P)), (a_lo, slice(0, P))]
                last = len(terms) - 1
                if k == 0:
                    steps = [(c, i, h) for c in range(CH) for i in range(len(terms)) for h in range(2)]
                else:
                    steps = [(c, i, h) for h in range(2) for c in range(CH) for i in range(len(terms))]
                for n, (c, i, h) in list(enumerate(steps))[start:stop]:
                    if n == 0 or (c == HC and i == 0 and h == 0):
                        pe.wait_ge(stat_ready[s], n_stat(k, c // HC, u))
                    if k == 2 and c == 0 and i == 0:
                        pe.wait_ge(rows_ready[s], n_half(h, u))
                    if k == 0 and c % 2 == 0 and i == 0 and h == 0:
                        pe.wait_ge(a_lo_ready[c // 2], batch(s, u) + 1)
                    src, at = terms[i]
                    ins = nc.tensor.matmul(agg[s][:, cols(h)], stat[s][:, c, at], src[s][:, c, cols(h)],
                                           start=(c == 0 and i == 0), stop=(c == CH - 1 and i == last))
                    if c == CH - 1 and i == last:
                        ins.then_inc(agg_done[s], 1)
                    elif k == 7 and h == 1 and c % 2 == 1 and i == last:
                        ins.then_inc(a_freed[s], 1)

            def stage(k, s, u, k0, s0, u0):
                first, second = DENSE_AT[k0, s0]
                aggregate(k, s, u, 0, first)
                first_dense(k0, s0, u0)
                if k == 0:
                    aggregate(k, s, u, first, XT_AT[s])
                    transpose_x(s, u)
                    aggregate(k, s, u, XT_AT[s], max(second, XT_AT[s]))
                    second_dense(k0, s0, u0)
                    aggregate(k, s, u, max(second, XT_AT[s]), X_TERM_AT)
                    x_term(s, u)
                    aggregate(k, s, u, X_TERM_AT, None)
                else:
                    aggregate(k, s, u, first, second)
                    second_dense(k0, s0, u0)
                    aggregate(k, s, u, second, None)

            pe.wait_ge(w_loaded, 16)
            nc.tensor.matmul(den[1][:, 0:P], stage_w[:, EMBED:EMBED + P], stage_w[:, ENC0:ENC0 + P],
                             start=True, stop=True).then_inc(w_product, 1)
            pe.wait_ge(w_ready, 1)
            aggregate(0, 0, 0, 0, XT_AT[0])
            transpose_x(0, 0)
            aggregate(0, 0, 0, XT_AT[0], X_TERM_AT)
            x_term(0, 0)
            aggregate(0, 0, 0, X_TERM_AT, None)
            pe.wait_ge(whole_loaded, 16)

            def pair(u, more):
                for (k0, s0), (k, s) in zip(ORDER, ORDER[1:]):
                    stage(k, s, u, k0, s0, u)
                if more:
                    stage(0, 0, u + 1, 7, 1, u)
                else:
                    first_dense(7, 1, u)

            with pe.Fori(0, PAIRS - 1) as u:
                pair(u, True)
            pair(PAIRS - 1, False)


def kernel(**inputs):
    import concourse.bacc as bacc
    from concourse.bass_utils import run_bass_kernel_spmd

    a = {k: np.asarray(v) for k, v in inputs.items()}

    def nodes(v):
        return np.ascontiguousarray(v.reshape(B, CH, P, -1).transpose(0, 2, 1, 3))

    def twice(v):
        return np.concatenate([v, v], axis=0)

    w1 = a["L0_gnn_W1"]
    parts = {
        "ones": np.ones((P, P), np.float32), "ident": np.eye(P, dtype=np.float32),
        "w1b": np.tile(w1[D:], (2, 2)), "w1a": np.tile(w1[:D], (2, 2)),
        "enc1": a["L2_gnn_Wl"][1], "enc2": a["L2_gnn_Wl"][2],
        "dec0": twice(a["L3_gnn_W0"]), "dec1": a["L3_gnn_W1"], "dec2": a["L3_gnn_W2"],
        "w2": np.concatenate([a["L0_gnn_W2"], np.zeros_like(a["L0_gnn_W2"])]), "gcn": twice(a["L1_gnn_weight"]),
        "proj": a["L2_gnn_W_proj"], "dout": a["L3_gnn_Wout"],
    }
    embed = a["L2_gnn_W_embed"].T
    weights = np.concatenate([parts[n] for n in EXACT + SPLIT] + [embed, embed, a["L2_gnn_Wl"][0]], axis=1)
    whole = np.concatenate([parts[n] for n in WIDE + NARROW], axis=1)
    along = [a["L2_gnn_bl"][1], a["L2_gnn_bl"][2], a["L3_gnn_b1"], a["L3_gnn_b2"],
             a["L0_gnn_b2"], a["L1_gnn_bias"], a["L2_gnn_b_proj"], a["L3_gnn_bout"]]
    down = [np.tile(a["L0_gnn_b1"], 2), a["L2_gnn_bl"][0], a["L3_gnn_b0"]]
    biases = np.concatenate([np.tile(np.concatenate(along), (P, 1)), np.stack(down, axis=1)], axis=1)
    arrays = {
        "x": nodes(a["x"]),
        "adj_t": nodes(a["adj"].transpose(0, 2, 1)),
        "mask": np.ascontiguousarray(a["nodemask"].reshape(B, CH, P).transpose(0, 2, 1)),
        "weights": np.ascontiguousarray(weights),
        "whole": np.ascontiguousarray(whole),
        "biases": np.ascontiguousarray(biases),
    }

    nc = bacc.Bacc("TRN2", target_bir_lowering=False, num_devices=1, dynamic_dma_scratch_size=1024)
    aps = {n: nc.dram_tensor(n, v.shape, mybir.dt.from_np(v.dtype), kind="ExternalInput").ap() for n, v in arrays.items()}
    out = nc.dram_tensor("out", (B, P, CH, D), F32, kind="ExternalOutput").ap()
    graph_networks(nc, aps["x"], aps["adj_t"], aps["mask"], aps["weights"], aps["whole"], aps["biases"], out)
    r = run_bass_kernel_spmd(nc, [arrays], core_ids=[0])
    return np.ascontiguousarray(r.results[0]["out"].transpose(0, 2, 1, 3)).reshape(B, N, D)
```

```python
from contextlib import ExitStack

import numpy as np

import concourse.bass as bass
from concourse import mybir


P = 128
B, N, D, HID = 8, 1024, 64, 128
CH = N // P
HALF = N // 2
HC = CH // 2
PAIRS = B // 2
SLOTS = CH // 2
EPS = 1e-5

F32 = mybir.dt.float32
F32R = mybir.dt.float32r
ALU = mybir.AluOpType
ACT = mybir.ActivationFunctionType
AX_X = mybir.AxisListType.X



def columns(widths):
    starts, at = {}, 0
    for name, width in widths.items():
        starts[name] = at
        at += width
    return starts


EXACT = ["ones"]
SPLIT = ["w1b", "dec0"]
WHOLE = {"w1a": P, "w2": D, "gcn": D, "proj": D, "dout": D, "enc1": HID, "enc2": HID, "dec1": HID, "dec2": HID}
N_EXACT = len(EXACT) * P
N_SPLIT = N_EXACT + len(SPLIT) * P
N_WHOLE = sum(WHOLE.values())
HI_COL = {n: i * P for i, n in enumerate(EXACT + SPLIT + ["enc0"])}
WHOLE_COL = columns(WHOLE)
EMBED, ENC0, N_STAGE = N_SPLIT, N_SPLIT + P, N_SPLIT + 2 * P
BIASES = {"tanh": 1, "enc0": 1, "dec0": 1, "w2": D, "gcn": D, "proj": D, "dout": D,
          "enc1": HID, "enc2": HID, "dec1": HID, "dec2": HID}
BCOL = columns(BIASES)
N_BIAS = sum(BIASES.values())
WHOLE_FIRST, BIAS_FIRST = WHOLE_COL["gcn"], BCOL["gcn"]

DENSE_AT = {(k, s): (6, 22) for k in range(8) for s in range(2)}
DENSE_AT |= {(0, 0): (8, 16), (0, 1): (3, 11), (7, 1): (12, 12), (1, 0): (5, 16), (1, 1): (5, 16)}
X_TERM_AT = (28, 2 * 2 * CH)

LN_OF = {0: 0, 1: 1, 4: 2, 7: 3}
LIFT_OF = {2: 0, 5: 1}
MSG_OF = {2: 0, 3: 1, 5: 2, 6: 3}
LIFT_W = {2: "enc0", 5: "dec0"}
MSG_W = {2: "enc1", 3: "enc2", 5: "dec1", 6: "dec2"}
NODE_W = {1: "gcn", 4: "proj", 7: "dout"}
NARROW_K = (0, 1, 2, 5)
ORDER = [(k, s) for k in range(8) for s in range(2)]
FILLS = [(k, s) for k in (0, 1, 2, 5) for s in range(2)]


def graph_networks(nc: bass.Bass, x, x_feat, adj_t, mask, weights, whole, biases, out):
    with ExitStack() as ctx:
        def sb(name, shape, dt=F32):
            return ctx.enter_context(nc.sbuf_tensor(name, shape, dt))

        def sem(name):
            return ctx.enter_context(nc.semaphore(name))

        def sems(name, n):
            return [sem(f"{name}{i}") for i in range(n)]

        a_hi = [sb(f"a_hi{s}", [P, CH, N], F32R) for s in range(2)]
        a_lo = [sb(f"a_lo{s}", [P, CH, N], F32R) for s in range(2)]
        raw = sb("raw", [P, CH, N])
        stat = [sb(f"stat{s}", [P, CH, 2 * HID], F32R) for s in range(2)]
        feat_hi = sb("feat_hi", [P, N], F32R)
        feat_lo = sb("feat_lo", [P, N], F32R)
        rows = [sb(f"rows{s}", [P, N]) for s in range(2)]
        work = [sb(f"work{s}", [P, N]) for s in range(2)]
        xn = [sb(f"xn{s}", [P, CH, D]) for s in range(2)]
        x_in = [sb(f"x_in{s}", [P, CH, D]) for s in range(2)]
        spare = sb("spare", [P, CH, D])
        xt = sb("xt", [P, HALF])
        mk = [sb(f"mk{s}", [P, CH]) for s in range(2)]
        w_hi = sb("w_hi", [P, N_SPLIT + P], F32R)
        w_lo = sb("w_lo", [P, N_SPLIT + P - N_EXACT], F32R)
        w_whole = sb("w_whole", [P, N_WHOLE])
        bias = sb("bias", [P, N_BIAS])
        ln_s = [sb(f"ln_s{s}", [P, CH]) for s in range(2)]
        ln_q = [sb(f"ln_q{s}", [P, CH]) for s in range(2)]
        ln_d = [sb(f"ln_d{s}", [P, CH]) for s in range(2)]
        ln_r = [sb(f"ln_r{s}", [P, CH]) for s in range(2)]
        eps = sb("eps", [P, 1])
        idle = sb("idle", [P, 1])
        eps_set = sem("eps_set")
        table_loaded = sem("table_loaded")
        stage_w = rows[1]
        y = [work[s][:, 0:HALF].rearrange("p (c d) -> p c d", d=D) for s in range(2)]
        sq = [work[s][:, HALF:N].rearrange("p (c d) -> p c d", d=D) for s in range(2)]

        agg = [ctx.enter_context(nc.psum_tensor(f"agg{s}", [P, N], F32)) for s in range(2)]
        den = [ctx.enter_context(nc.psum_tensor(f"den{s}", [P, N], F32)) for s in range(2)]

        w_loaded = sem("w_loaded")
        w_rounded = sem("w_rounded")
        w_product = sem("w_product")
        w_ready = sem("w_ready")
        whole_loaded = sem("whole_loaded")
        bias_loaded = sem("bias_loaded")
        whole_rest_loaded = sem("whole_rest_loaded")
        bias_rest_loaded = sem("bias_rest_loaded")
        x_loaded = sems("x_loaded", 2)
        mask_loaded = sems("mask_loaded", 2)
        raw_loaded = sems("raw_loaded", SLOTS)
        out_stored = sem("out_stored")
        a_freed = sems("a_freed", 2)
        a_hi_ready = sems("a_hi_ready", SLOTS)
        a_lo_ready = sems("a_lo_ready", SLOTS)
        rows_added = sem("rows_added")
        bias_masked = sem("bias_masked")
        xb_ready = sems("xb_ready", 2)
        agg_done = sems("agg_done", 2)
        pre_done = sems("pre_done", 2)
        node_done = sems("node_done", 2)
        rows_done = sems("rows_done", 2)
        lift_done = sems("lift_done", 2)
        msg_done = sems("msg_done", 2)
        xt_loaded = sems("xt_loaded", 2)
        work_ready = sems("work_ready", 2)
        feat_hi_ready = sem("feat_hi_ready")
        feat_lo_ready = sem("feat_lo_ready")
        rows_ready = sems("rows_ready", 2)
        lifted = sems("lifted", 2)
        msg_biased = sems("msg_biased", 2)
        stat_hi_ready = sems("stat_hi_ready", 2)
        stat_ready = sems("stat_ready", 2)
        y_masked = sem("y_masked")
        y_done = sems("y_done", 2)
        ln_sum = sems("ln_sum", 2)
        ln_centered = sems("ln_centered", 2)
        ln_squared = sems("ln_squared", 2)
        ln_sqsum = sems("ln_sqsum", 2)
        ln_std = sems("ln_std", 2)
        ln_rstd = sems("ln_rstd", 2)
        ln_scaled = sems("ln_scaled", 2)

        def begins(u):
            return isinstance(u, int) and u == 0

        def batch(s, u):
            return u * 2 + s

        def n_agg(k, h, u):
            return u * 16 + (2 * k + h + 1)

        def n_stat(k, h, u):
            return u * 16 + (2 * k + h + 1)

        def n_residual(k, u):
            return u * 4 + (LN_OF[k] + 1)

        def n_node(k, h, u):
            return u * 8 + (2 * LN_OF[k] + h + 1)

        def n_work(k, h, u):
            return u * 16 + (2 * k + h + 1)

        def n_half(h, u):
            return u * 2 + (h + 1)

        def n_lift(k, h, u):
            return u * 4 + (2 * LIFT_OF[k] + h + 1)

        def n_msg(k, h, u):
            return u * 8 + (2 * MSG_OF[k] + h + 1)


        def n_fill(k, s, h, u):
            return u * (2 * len(FILLS)) + (2 * FILLS.index((k, s)) + h + 1)

        def cols(h):
            return slice(h * HALF, (h + 1) * HALF)

        def per_node(a, h=None):
            if h is None:
                return a.unsqueeze(2).to_broadcast([P, CH, D])
            return a[:, h * HC:(h + 1) * HC].unsqueeze(2).to_broadcast([P, HC, D])

        def per_feature(name):
            return bias[:, BCOL[name]:BCOL[name] + D].unsqueeze(1).to_broadcast([P, CH, D])

        def stat_hi(s, k, h):
            return stat[s][:, h * HC:(h + 1) * HC, 0:D if k in NARROW_K else HID]

        def stat_lo(s, k, h):
            w = D if k in NARROW_K else HID
            return stat[s][:, h * HC:(h + 1) * HC, w:2 * w]

        def chunks(h):
            return slice(h * HC, (h + 1) * HC)

        def half_of(a, h):
            return a[:, h * HC:(h + 1) * HC, :]

        def node_form(a, h):
            return a[:, cols(h)].rearrange("p (c n) -> p c n", n=HID)

        block = ctx.enter_context(nc.Block())

        @block.sync
        def _(sp):
            def load_raw(s, u, slots=range(SLOTS)):
                b = batch(s, u)
                empty = s == 0 and begins(u)
                if not empty and slots[0] == 0:
                    sp.wait_ge(a_lo_ready[0], b)
                for j in slots:
                    if not empty:
                        sp.wait_ge(rows_added, (b - 1) * (CH - 1) + (2 * j + 1))
                        if j > 0:
                            sp.wait_ge(a_lo_ready[j], b)
                    sp.dma_start(raw[:, 2 * j:2 * j + 2, :], adj_t[b, :, 2 * j:2 * j + 2, :]).then_inc(raw_loaded[j], 16)

            def load_x(s, u):
                if not begins(u):
                    sp.wait_ge(xb_ready[s], n_residual(0, u - 1))
                    sp.wait_ge(stat_ready[s], n_stat(0, 1, u - 1))
                sp.dma_start(x_in[s][:], x[batch(s, u)]).then_inc(x_loaded[s], 16)

            def load_x_features(s, u):
                if s == 1:
                    sp.wait_ge(pre_done[0], n_half(1, u))
                elif not begins(u):
                    sp.wait_ge(pre_done[1], n_half(1, u - 1))
                sp.dma_start(xt[:], x_feat[batch(s, u)]).then_inc(xt_loaded[s], 16)

            def load_mask(s, u):
                if not begins(u):
                    sp.wait_ge(out_stored, (batch(s, u) - 1) * 16)
                sp.dma_start(mk[s][:], mask[batch(s, u)]).then_inc(mask_loaded[s], 16)

            def store(s, u):
                sp.wait_ge(ln_scaled[s], n_node(7, 1, u))
                sp.dma_start(out[batch(s, u)], spare[:]).then_inc(out_stored, 16)

            load_x(0, 0)
            load_raw(0, 0)
            load_x(1, 0)
            load_raw(1, 0, slots=range(0, 1))
            sp.dma_start(stage_w[:, 0:N_STAGE], weights).then_inc(w_loaded, 16)
            sp.dma_start(bias[:, 0:BIAS_FIRST], biases[:, 0:BIAS_FIRST]).then_inc(bias_loaded, 16)
            sp.dma_start(w_whole[:, 0:WHOLE_FIRST], whole[:, 0:WHOLE_FIRST]).then_inc(whole_loaded, 16)
            load_x_features(0, 0)
            load_raw(1, 0, slots=range(1, SLOTS))
            sp.dma_start(w_whole[:, WHOLE_FIRST:], whole[:, WHOLE_FIRST:]).then_inc(whole_rest_loaded, 16)
            sp.dma_start(bias[:, BIAS_FIRST:], biases[:, BIAS_FIRST:]).then_inc(bias_rest_loaded, 16)
            load_x_features(1, 0)
            load_mask(0, 0)
            load_mask(1, 0)

            def pair(u, more):
                if more:
                    load_raw(0, u + 1)
                    for s in range(2):
                        load_x(s, u + 1)
                    load_x_features(0, u + 1)
                    load_raw(1, u + 1)
                store(0, u)
                if more:
                    load_mask(0, u + 1)
                    load_x_features(1, u + 1)
                store(1, u)
                if more:
                    load_mask(1, u + 1)

            with sp.Fori(0, PAIRS - 1) as u:
                pair(u, True)
            pair(PAIRS - 1, False)
            sp.wait_ge(out_stored, 16 * B)

        @block.gpsimd
        def _(pool):
            def add_rows(s, u, j):
                b = batch(s, u)
                pool.wait_ge(raw_loaded[j], (b + 1) * 16)
                at = b * (CH - 1) + 2 * j
                if j == 0:
                    if not begins(u):
                        pool.wait_ge(lifted[s], u * 4)
                    elif s == 1:
                        pool.wait_ge(w_ready, 1)
                    nc.gpsimd.tensor_tensor(rows[s][:], raw[:, 0], raw[:, 1], ALU.add).then_inc(rows_added, 1)
                    return
                for c in range(2):
                    pool.wait_ge(rows_added, at - 1 + c)
                    nc.gpsimd.tensor_tensor(rows[s][:], rows[s][:], raw[:, 2 * j + c], ALU.add).then_inc(rows_added, 1)

            def residual0(s, u):
                if begins(u):
                    pool.wait_ge(bias_loaded, 16)
                pool.wait_ge(x_loaded[s], (u + 1) * 16)
                if not begins(u):
                    pool.wait_ge(y_done[s], u * 8)
                nc.gpsimd.tensor_tensor(xn[s][:], x_in[s][:], per_feature("w2"), ALU.add).then_inc(xb_ready[s], 1)

            def take_batch(s, u):
                j = SLOTS - 1
                if s == 0:
                    for i in range(SLOTS):
                        add_rows(s, u, i)
                if not begins(u):
                    pool.wait_ge(a_hi_ready[j], batch(s, u) + 1)
                    nc.gpsimd.tensor_tensor(a_lo[s][:, 2 * j:2 * j + 2], raw[:, 2 * j:2 * j + 2],
                                            a_hi[s][:, 2 * j:2 * j + 2].bitcast(F32), ALU.subtract).then_inc(a_lo_ready[j], 1)
                residual0(s, u)
                if s == 1:
                    for i in range(SLOTS):
                        add_rows(s, u, i)

            def residual(s, u, k):
                if k > 0:
                    n = u * 4 + (2 * (LN_OF[k] - 1) + s + 1)
                    for r in range(2):
                        pool.wait_ge(mask_loaded[r], (u + 1) * 16)
                    pool.wait_ge(xb_ready[1 - s], n_residual(k, u) + s)
                    nc.gpsimd.tensor_tensor(spare[:], per_node(mk[s][:]), per_feature("proj" if k == 1 else "dout"),
                                            ALU.mult).then_inc(bias_masked, 1)
                    pool.wait_ge(bias_masked, n)
                pool.wait_ge(stat_ready[s], n_stat(k + 1, 1, u))
                term = per_feature("gcn") if k == 0 else spare[:]
                nc.gpsimd.tensor_tensor(xn[s][:], xn[s][:], term, ALU.add).then_inc(xb_ready[s], 1)

            take_batch(0, 0)
            take_batch(1, 0)
            pool.wait_ge(bias_rest_loaded, 16)

            def pair(u, more):
                for k in (0, 1, 4):
                    for s in range(2):
                        residual(s, u, k)
                if more:
                    for s in range(2):
                        take_batch(s, u + 1)

            with pool.Fori(0, PAIRS - 1) as u:
                pair(u, True)
            pair(PAIRS - 1, False)

        @block.scalar
        def _(act):
            def split_adj(s, u, freed, slots=range(SLOTS)):
                b = batch(s, u)
                for j in slots:
                    act.wait_ge(raw_loaded[j], (b + 1) * 16)
                    if freed is not None:
                        if j < SLOTS - 1:
                            act.wait_ge(a_freed[s], freed * (SLOTS - 1) + (j + 1))
                        else:
                            act.wait_ge(agg_done[s], n_agg(7, 1, freed))
                    nc.scalar.activation(a_hi[s][:, 2 * j:2 * j + 2], raw[:, 2 * j:2 * j + 2], ACT.Copy).then_inc(a_hi_ready[j], 1)

            def round_x(s, u, last):
                act.wait_ge(x_loaded[s], (u + 1) * 16)
                if last is not None:
                    act.wait_ge(agg_done[s], n_agg(7, 1, last))
                for h in range(2):
                    nc.scalar.activation(stat_hi(s, 0, h), half_of(x_in[s], h), ACT.Copy).then_inc(stat_hi_ready[s], 1)

            def fill(k, s, u):
                for h in range(2):
                    if k == 0 and s == 0:
                        if not begins(u):
                            act.wait_ge(lift_done[1], (u - 1) * 4 + (2 * LIFT_OF[5] + h + 1))
                    elif k == 0:
                        act.wait_ge(pre_done[0], n_half(h, u))
                    elif k == 1 and s == 0:
                        act.wait_ge(pre_done[1], n_half(h, u))
                    elif k == 1:
                        act.wait_ge(rows_done[0], n_half(h, u))
                    elif k == 2 and s == 0:
                        act.wait_ge(rows_done[1], n_half(h, u))
                    elif s == 1:
                        act.wait_ge(lift_done[0], n_lift(k, h, u))
                    else:
                        act.wait_ge(lift_done[1], n_lift(2, h, u))
                    if k == 1:
                        act.wait_ge(rows_added, (batch(s, u) + 1) * (CH - 1))
                        source = rows[s]
                    else:
                        act.wait_ge(agg_done[s], n_agg(k, h, u))
                        source = agg[s]
                    nc.scalar.activation(feat_hi[:, cols(h)], source[:, cols(h)], ACT.Copy).then_inc(feat_hi_ready, 1)

            def take_aggregate(k, s, u):
                for h in range(2):
                    act.wait_ge(agg_done[s], n_agg(k, h, u))
                    nc.scalar.activation(work[s][:, cols(h)], agg[s][:, cols(h)],
                                         ACT.Copy if k == 1 else ACT.Relu).then_inc(work_ready[s], 1)

            def n_table(back, s, u):
                return u * 4 + (2 * s + back + 1)

            def load_table(fn, loads):
                act.wait_ge(table_loaded, loads)
                nc.scalar.activation(idle[:], eps[:], fn).then_inc(table_loaded, 1)

            def square(k, s, u, h):
                act.wait_ge(ln_centered[s], n_node(k, h, u))
                nc.scalar.activation(half_of(sq[s], h), half_of(y[s], h), ACT.Square).then_inc(ln_squared[s], 1)

            def root(k, s, u, h):
                act.wait_ge(ln_sqsum[s], n_node(k, h, u))
                nc.scalar.activation(ln_d[s][:, chunks(h)], ln_q[s][:, chunks(h)], ACT.Sqrt, bias=eps[:, 0:1],
                                     scale=1.0 / D).then_inc(ln_std[s], 1)

            def round_xn(k, s, u, h):
                act.wait_ge(ln_scaled[s], n_node(k, h, u))
                nc.scalar.activation(stat_hi(s, k + 1, h), half_of(xn[s], h), ACT.Copy).then_inc(stat_hi_ready[s], 1)

            def norm(k, s, u):
                for h in range(2):
                    square(k, s, u, h)
                for h in range(2):
                    root(k, s, u, h)
                if k < 7:
                    for h in range(2):
                        round_xn(k, s, u, h)

            def tanh(s, u):
                if s == 0:
                    load_table(ACT.Tanh, n_table(0, s, u))
                for h in range(2):
                    act.wait_ge(pre_done[s], n_half(h, u))
                    nc.scalar.activation(work[s][:, cols(h)], den[s][:, cols(h)], ACT.Tanh,
                                         bias=bias[:, BCOL["tanh"]:BCOL["tanh"] + 1]).then_inc(work_ready[s], 1)

            def finish(k, s, u):
                if k == 0:
                    tanh(s, u)
                    load_table(ACT.Sqrt, n_table(1, s, u))
                elif k in LIFT_OF:
                    fill(k, s, u)
                    for h in range(2):
                        act.wait_ge(lifted[s], n_lift(k, h, u))
                        nc.scalar.activation(work[s][:, cols(h)], work[s][:, cols(h)], ACT.Relu).then_inc(work_ready[s], 1)
                else:
                    take_aggregate(k, s, u)
                if k == 1:
                    fill(k, s, u)
                if k in MSG_OF:
                    for h in range(2):
                        act.wait_ge(msg_biased[s], n_msg(k, h, u))
                        nc.scalar.activation(stat_hi(s, k + 1, h), node_form(work[s], h), ACT.Copy).then_inc(stat_hi_ready[s], 1)

            def take_rows(s, u):
                for h in range(2):
                    act.wait_ge(rows_done[s], n_half(h, u))
                    nc.scalar.activation(rows[s][:, cols(h)], agg[s][:, cols(h)], ACT.Copy).then_inc(rows_ready[s], 1)

            act.wait_ge(eps_set, 1)
            nc.scalar.activation(idle[:], eps[:], ACT.Tanh).then_inc(table_loaded, 1)
            round_x(0, 0, None)
            split_adj(0, 0, None)
            round_x(1, 0, None)
            split_adj(1, 0, None, range(0, 1))
            fill(0, 0, 0)
            split_adj(1, 0, None, range(1, 3))
            act.wait_ge(bias_loaded, 16)
            tanh(0, 0)
            split_adj(1, 0, None, range(3, SLOTS))
            load_table(ACT.Sqrt, n_table(1, 0, 0))
            norm(0, 0, 0)
            fill(0, 1, 0)
            load_table(ACT.Tanh, n_table(0, 1, 0))

            def pair(u, more):
                finish(0, 1, u)
                norm(0, 1, u)
                for k, s in ORDER[2:-2]:
                    finish(k, s, u)
                    if k in LN_OF:
                        norm(k, s, u)
                    if k == 1:
                        take_rows(s, u)
                finish(7, 0, u)
                if more:
                    split_adj(0, u + 1, u)
                    round_x(0, u + 1, u)
                norm(7, 0, u)
                finish(7, 1, u)
                if more:
                    split_adj(1, u + 1, u, range(0, 1))
                    round_x(1, u + 1, u)
                    split_adj(1, u + 1, u, range(1, SLOTS))
                    fill(0, 0, u + 1)
                    finish(0, 0, u + 1)
                    for h in range(2):
                        square(7, 1, u, h)
                    norm(0, 0, u + 1)
                    fill(0, 1, u + 1)
                    for h in range(2):
                        root(7, 1, u, h)
                    load_table(ACT.Tanh, n_table(0, 1, u + 1))
                    act.wait_ge(ln_scaled[1], n_node(7, 1, u))
                else:
                    norm(7, 1, u)

            with act.Fori(0, PAIRS - 1) as u:
                pair(u, True)
            pair(PAIRS - 1, False)

        @block.vector
        def _(dve):
            def split_adj(s, u, slots=range(SLOTS - 1)):
                b = batch(s, u)
                for j in slots:
                    dve.wait_ge(a_hi_ready[j], b + 1)
                    nc.vector.tensor_tensor(a_lo[s][:, 2 * j:2 * j + 2], raw[:, 2 * j:2 * j + 2],
                                            a_hi[s][:, 2 * j:2 * j + 2].bitcast(F32), ALU.subtract).then_inc(a_lo_ready[j], 1)

            def split_stat(s, u, k, source, h):
                dve.wait_ge(stat_hi_ready[s], n_stat(k, h, u))
                nc.vector.tensor_tensor(stat_lo(s, k, h), source, stat_hi(s, k, h).bitcast(F32),
                                        ALU.subtract).then_inc(stat_ready[s], 1)

            def split_x(s, u):
                for h in range(2):
                    split_stat(s, u, 0, half_of(x_in[s], h), h)

            def fill(k, s, u):
                for h in range(2):
                    dve.wait_ge(feat_hi_ready, n_fill(k, s, h, u))
                    nc.vector.tensor_tensor(feat_lo[:, cols(h)], (rows if k == 1 else agg)[s][:, cols(h)],
                                            feat_hi[:, cols(h)].bitcast(F32), ALU.subtract).then_inc(feat_lo_ready, 1)

            def add_row_bias(k, s, u):
                b = BCOL[LIFT_W[k]]
                for h in range(2):
                    if k == 2:
                        dve.wait_ge(rows_ready[s], n_half(h, u))
                    dve.wait_ge(lift_done[s], n_lift(k, h, u))
                    nc.vector.scalar_tensor_tensor(out=work[s][:, cols(h)], in0=rows[s][:, cols(h)], scalar=bias[:, b:b + 1],
                                                   in1=den[s][:, cols(h)], op0=ALU.mult, op1=ALU.add).then_inc(lifted[s], 1)

            def add_msg_bias(k, s, u):
                source = agg[s] if k in LIFT_OF else den[s]
                b = BCOL[MSG_W[k]]
                b_all = bias[:, b:b + HID].unsqueeze(1).to_broadcast([P, HC, HID])
                for h in range(2):
                    dve.wait_ge(msg_done[s], n_msg(k, h, u))
                    nc.vector.tensor_tensor(node_form(work[s], h), node_form(source, h), b_all, ALU.add).then_inc(msg_biased[s], 1)
                for h in range(2):
                    split_stat(s, u, k + 1, node_form(work[s], h), h)

            def network_out(k, s, h):
                return (agg if k == 0 else den)[s][:, h * HALF:h * HALF + HC * D].rearrange("p (c d) -> p c d", d=D)

            def mask_out(k, s, u):
                dve.wait_ge(mask_loaded[s], (u + 1) * 16)
                for h in range(2):
                    dve.wait_ge(node_done[s], n_node(k, h, u))
                    nc.vector.tensor_tensor(half_of(y[s], h), network_out(k, s, h), per_node(mk[s], h), ALU.mult).then_inc(y_masked, 1)

            def center(k, s, u):
                dve.wait_ge(xb_ready[s], n_residual(k, u))
                for h in range(2):
                    if k >= 4:
                        dve.wait_ge(y_masked, u * 8 + (4 * (LN_OF[k] - 2) + 2 * s + h + 2))
                        nc.vector.tensor_tensor(half_of(y[s], h), half_of(y[s], h), half_of(xn[s], h), ALU.add).then_inc(y_done[s], 1)
                    else:
                        dve.wait_ge(node_done[s], n_node(k, h, u))
                        nc.vector.tensor_tensor(half_of(y[s], h), network_out(k, s, h), half_of(xn[s], h), ALU.add).then_inc(y_done[s], 1)
                for h in range(2):
                    dve.wait_ge(y_done[s], n_node(k, h, u))
                    nc.vector.tensor_reduce(ln_s[s][:, chunks(h)], half_of(y[s], h), AX_X, ALU.add).then_inc(ln_sum[s], 1)
                for h in range(2):
                    dve.wait_ge(ln_sum[s], n_node(k, h, u))
                    nc.vector.scalar_tensor_tensor(out=half_of(y[s], h), in0=per_node(ln_s[s], h), scalar=-1.0 / D, in1=half_of(y[s], h),
                                                   op0=ALU.mult, op1=ALU.add).then_inc(ln_centered[s], 1)

            def scale(k, s, u):
                for h in range(2):
                    dve.wait_ge(ln_squared[s], n_node(k, h, u))
                    nc.vector.tensor_reduce(ln_q[s][:, chunks(h)], half_of(sq[s], h), AX_X, ALU.add).then_inc(ln_sqsum[s], 1)
                if k == 7:
                    if s == 0:
                        dve.wait_ge(mask_loaded[1], (u + 1) * 16)
                    else:
                        dve.wait_ge(out_stored, batch(0, u) * 16 + 16)
                    for r in range(2):
                        dve.wait_ge(xb_ready[r], n_residual(7, u))
                for h in range(2):
                    dve.wait_ge(ln_std[s], n_node(k, h, u))
                    nc.vector.reciprocal(ln_r[s][:, chunks(h)], ln_d[s][:, chunks(h)]).then_inc(ln_rstd[s], 1)
                for h in range(2):
                    dve.wait_ge(ln_rstd[s], n_node(k, h, u))
                    nc.vector.tensor_tensor(half_of(spare if k == 7 else xn[s], h), half_of(y[s], h), per_node(ln_r[s], h),
                                            ALU.mult).then_inc(ln_scaled[s], 1)

            def norm(k, s, u):
                if k >= 4:
                    mask_out(k, s, u)
                center(k, s, u)
                scale(k, s, u)
                if k < 7:
                    for h in range(2):
                        split_stat(s, u, k + 1, half_of(xn[s], h), h)

            def finish(k, s, u):
                if k in (1, 2, 5):
                    fill(k, s, u)
                if k in LIFT_OF:
                    add_row_bias(k, s, u)
                if k in MSG_OF:
                    add_msg_bias(k, s, u)
                if k in LN_OF:
                    norm(k, s, u)

            nc.vector.memset(eps[:], EPS).then_inc(eps_set, 1)
            nc.vector.memset(ln_s[0][:], 0.0).then_inc(y_masked, 1)
            dve.wait_ge(x_loaded[0], 16)
            split_x(0, 0)
            split_adj(0, 0, range(SLOTS))
            dve.wait_ge(x_loaded[1], 16)
            split_x(1, 0)
            dve.wait_ge(w_loaded, 16)
            nc.vector.tensor_copy(w_hi[:, 0:N_SPLIT], stage_w[:, 0:N_SPLIT]).then_inc(w_rounded, 1)
            dve.wait_ge(w_rounded, 1)
            nc.vector.tensor_tensor(w_lo[:, 0:N_SPLIT - N_EXACT], stage_w[:, N_EXACT:N_SPLIT],
                                    w_hi[:, N_EXACT:N_SPLIT].bitcast(F32), ALU.subtract)
            dve.wait_ge(w_product, 1)
            nc.vector.tensor_copy(w_hi[:, N_SPLIT:N_SPLIT + P], den[1][:, 0:P]).then_inc(w_rounded, 1)
            dve.wait_ge(w_rounded, 2)
            nc.vector.tensor_tensor(w_lo[:, N_SPLIT - N_EXACT:], den[1][:, 0:P], w_hi[:, N_SPLIT:N_SPLIT + P].bitcast(F32),
                                    ALU.subtract).then_inc(w_ready, 1)
            split_adj(1, 0, range(0, 1))
            fill(0, 0, 0)
            split_adj(1, 0, range(1, SLOTS))
            norm(0, 0, 0)
            fill(0, 1, 0)
            dve.wait_ge(bias_rest_loaded, 16)

            def pair(u, more):
                norm(0, 1, u)
                for k, s in ORDER[2:-2]:
                    finish(k, s, u)
                if more:
                    split_adj(0, u + 1)
                    split_x(0, u + 1)
                norm(7, 0, u)
                if more:
                    split_adj(1, u + 1, range(0, 1))
                    split_x(1, u + 1)
                    split_adj(1, u + 1, range(1, SLOTS - 1))
                    fill(0, 0, u + 1)
                    mask_out(7, 1, u)
                    center(7, 1, u)
                    norm(0, 0, u + 1)
                    fill(0, 1, u + 1)
                    scale(7, 1, u)
                else:
                    norm(7, 1, u)

            with dve.Fori(0, PAIRS - 1) as u:
                pair(u, True)
            pair(PAIRS - 1, False)

        @block.tensor
        def _(pe):
            def w(part, name):
                at = HI_COL[name] - (N_EXACT if part is w_lo else 0)
                return part[:, at:at + P]

            def feature_layer(target, terms, h, start=True, stop=True):
                for i, (wt, src) in enumerate(terms):
                    ins = nc.tensor.matmul(target[:, cols(h)], wt, src[:, cols(h)],
                                           start=(start and i == 0), stop=(stop and i == len(terms) - 1))
                return ins

            def split_terms(name):
                return [(w(w_hi, name), feat_hi), (w(w_hi, name), feat_lo), (w(w_lo, name), feat_hi)]

            def node_layer(target, s, name, width, h):
                at = WHOLE_COL[name]
                for i in range(HC):
                    c, out_at = h * HC + i, h * HALF + i * width
                    ins = nc.tensor.matmul(target[:, out_at:out_at + width], work[s][:, c * P:(c + 1) * P],
                                           w_whole[:, at:at + width], start=True, stop=True)
                return ins

            def first_dense(k, s, u):
                if k == 1:
                    pe.wait_ge(whole_rest_loaded, 16)
                for h in range(2):
                    if k == 0:
                        pe.wait_ge(feat_lo_ready, n_fill(k, s, h, u))
                        feature_layer(den[s], split_terms("w1b"), h, start=False).then_inc(pre_done[s], 1)
                    elif k in LIFT_OF:
                        pe.wait_ge(feat_lo_ready, n_fill(k, s, h, u))
                        feature_layer(den[s], split_terms(LIFT_W[k]), h).then_inc(lift_done[s], 1)
                    elif k in MSG_OF:
                        pe.wait_ge(work_ready[s], n_work(k, h, u))
                        node_layer(den[s], s, MSG_W[k], HID, h).then_inc(msg_done[s], 1)
                    else:
                        pe.wait_ge(work_ready[s], n_work(k, h, u))
                        node_layer(den[s], s, NODE_W[k], D, h).then_inc(node_done[s], 1)

            def second_dense(k, s, u):
                for h in range(2):
                    if k == 0:
                        pe.wait_ge(work_ready[s], n_work(k, h, u))
                        node_layer(agg[s], s, "w2", D, h).then_inc(node_done[s], 1)
                    elif k == 1:
                        pe.wait_ge(feat_lo_ready, n_fill(k, s, h, u))
                        feature_layer(agg[s], [(w(w_hi, "ones"), feat_hi), (w(w_hi, "ones"), feat_lo)], h).then_inc(rows_done[s], 1)
                    elif k in LIFT_OF:
                        pe.wait_ge(work_ready[s], n_work(k, h, u))
                        node_layer(agg[s], s, MSG_W[k], HID, h).then_inc(msg_done[s], 1)

            def x_term(s, u):
                pe.wait_ge(xt_loaded[s], (u + 1) * 16)
                if s == 1:
                    pe.wait_ge(y_masked, u * 8 + 1)
                elif not begins(u):
                    pe.wait_ge(y_masked, u * 8 - 1)
                at = WHOLE_COL["w1a"]
                for h in range(2):
                    on = slice(h * D, (h + 1) * D)
                    nc.tensor.matmul(den[s][:, cols(h)], w_whole[on, at:at + P], xt[on, :], start=True, stop=False)

            def aggregate(k, s, u, start, stop):
                if k in NARROW_K:
                    terms = [(a_hi, slice(0, P)), (a_lo, slice(0, P))]
                else:
                    terms = [(a_hi, slice(0, P)), (a_hi, slice(P, 2 * P)), (a_lo, slice(0, P))]
                last = len(terms) - 1
                if k == 0:
                    steps = [(c, i, h) for c in range(CH) for i in range(len(terms)) for h in range(2)]
                else:
                    steps = [(c, i, h) for h in range(2) for c in range(CH) for i in range(len(terms))]
                for n, (c, i, h) in list(enumerate(steps))[start:stop]:
                    if n == 0 or (c == HC and i == 0 and h == 0):
                        pe.wait_ge(stat_ready[s], n_stat(k, c // HC, u))
                    if k == 2 and c == 0 and i == 0:
                        pe.wait_ge(rows_ready[s], n_half(h, u))
                    if k == 0 and c % 2 == 0 and i == 0 and h == 0:
                        pe.wait_ge(a_lo_ready[c // 2], batch(s, u) + 1)
                    src, at = terms[i]
                    ins = nc.tensor.matmul(agg[s][:, cols(h)], stat[s][:, c, at], src[s][:, c, cols(h)],
                                           start=(c == 0 and i == 0), stop=(c == CH - 1 and i == last))
                    if c == CH - 1 and i == last:
                        ins.then_inc(agg_done[s], 1)
                    elif k == 7 and h == 1 and c % 2 == 1 and i == last:
                        ins.then_inc(a_freed[s], 1)

            def stage(k, s, u, k0, s0, u0):
                first, second = DENSE_AT[k0, s0]
                aggregate(k, s, u, 0, first)
                first_dense(k0, s0, u0)
                aggregate(k, s, u, first, second)
                second_dense(k0, s0, u0)
                if k == 0:
                    aggregate(k, s, u, second, X_TERM_AT[s])
                    x_term(s, u)
                    aggregate(k, s, u, X_TERM_AT[s], None)
                else:
                    aggregate(k, s, u, second, None)

            aggregate(0, 0, 0, 0, None)
            pe.wait_ge(w_loaded, 16)
            nc.tensor.matmul(den[1][:, 0:P], stage_w[:, EMBED:EMBED + P], stage_w[:, ENC0:ENC0 + P],
                             start=True, stop=True).then_inc(w_product, 1)
            pe.wait_ge(whole_loaded, 16)
            x_term(0, 0)
            pe.wait_ge(w_ready, 1)

            def pair(u, more):
                for (k0, s0), (k, s) in zip(ORDER, ORDER[1:]):
                    stage(k, s, u, k0, s0, u)
                if more:
                    stage(0, 0, u + 1, 7, 1, u)
                else:
                    first_dense(7, 1, u)

            with pe.Fori(0, PAIRS - 1) as u:
                pair(u, True)
            pair(PAIRS - 1, False)


def kernel(**inputs):
    import concourse.bacc as bacc
    from concourse.bass_utils import run_bass_kernel_spmd

    a = {k: np.asarray(v) for k, v in inputs.items()}

    def nodes(v):
        return np.ascontiguousarray(v.reshape(B, CH, P, -1).transpose(0, 2, 1, 3))

    def twice(v):
        return np.concatenate([v, v], axis=0)

    w1 = a["L0_gnn_W1"]
    parts = {
        "ones": np.ones((P, P), np.float32),
        "w1b": np.tile(w1[D:], (2, 2)), "w1a": np.tile(w1[:D], (2, 2)),
        "enc1": a["L2_gnn_Wl"][1], "enc2": a["L2_gnn_Wl"][2],
        "dec0": twice(a["L3_gnn_W0"]), "dec1": a["L3_gnn_W1"], "dec2": a["L3_gnn_W2"],
        "w2": np.concatenate([a["L0_gnn_W2"], np.zeros_like(a["L0_gnn_W2"])]), "gcn": twice(a["L1_gnn_weight"]),
        "proj": a["L2_gnn_W_proj"], "dout": a["L3_gnn_Wout"],
    }
    embed = a["L2_gnn_W_embed"].T
    weights = np.concatenate([parts[n] for n in EXACT + SPLIT] + [embed, embed, a["L2_gnn_Wl"][0]], axis=1)
    whole = np.concatenate([parts[n] for n in WHOLE], axis=1)
    along = [a["L0_gnn_b2"], a["L1_gnn_bias"], a["L2_gnn_b_proj"], a["L3_gnn_bout"],
             a["L2_gnn_bl"][1], a["L2_gnn_bl"][2], a["L3_gnn_b1"], a["L3_gnn_b2"]]
    down = [np.tile(a["L0_gnn_b1"], 2), a["L2_gnn_bl"][0], a["L3_gnn_b0"]]
    biases = np.concatenate([np.stack(down, axis=1), np.tile(np.concatenate(along), (P, 1))], axis=1)
    arrays = {
        "x": nodes(a["x"]),
        "x_feat": np.ascontiguousarray(a["x"].reshape(B, 2, HALF, D).transpose(0, 1, 3, 2).reshape(B, P, HALF)),
        "adj_t": nodes(a["adj"].transpose(0, 2, 1)),
        "mask": np.ascontiguousarray(a["nodemask"].reshape(B, CH, P).transpose(0, 2, 1)),
        "weights": np.ascontiguousarray(weights),
        "whole": np.ascontiguousarray(whole),
        "biases": np.ascontiguousarray(biases),
    }

    nc = bacc.Bacc("TRN2", target_bir_lowering=False, num_devices=1, dynamic_dma_scratch_size=1024)
    aps = {n: nc.dram_tensor(n, v.shape, mybir.dt.from_np(v.dtype), kind="ExternalInput").ap() for n, v in arrays.items()}
    out = nc.dram_tensor("out", (B, P, CH, D), F32, kind="ExternalOutput").ap()
    graph_networks(nc, aps["x"], aps["x_feat"], aps["adj_t"], aps["mask"], aps["weights"], aps["whole"], aps["biases"], out)
    r = run_bass_kernel_spmd(nc, [arrays], core_ids=[0])
    return np.ascontiguousarray(r.results[0]["out"].transpose(0, 2, 1, 3)).reshape(B, N, D)
```
